# Optimizing a Trainium2 kernel written in Bass

```python
import numpy as np
import jax
import jax.numpy as jnp

def _softmax(x, axis=-1):
    return jax.nn.softmax(x, axis=axis)

def _gelu(x):
    return jax.nn.gelu(x, approximate=True)

def _silu(x):
    return jax.nn.silu(x)

def _sigmoid(x):
    return jax.nn.sigmoid(x)

def _layernorm(x, axis=-1, eps=1e-05):
    m = jnp.mean(x, axis=axis, keepdims=True)
    v = jnp.var(x, axis=axis, keepdims=True)
    return (x - m) / jnp.sqrt(v + eps)

def _scatter_add(tgt, idx, src, axis=0):
    return tgt.at[idx].add(src)

def _segment_sum(src, seg, n):
    return jax.ops.segment_sum(src, seg, n)
kernel_name = 'mk_flamingo_gated_d1_seqx_r4_82eb49'

def setup_inputs(seed: int=0):
    np.random.seed(seed)
    _w = jnp.asarray

    def _rec_inputs():
        import jax
        import jax.numpy as jnp
        _rk = jax.random.key(seed)
        x = -0.0002928 + 1 * jax.random.normal(jax.random.fold_in(_rk, 1), (64, 128, 256), jnp.float32)
        _lenS = 128 - jax.random.randint(jax.random.fold_in(_rk, 7), (64,), 0, max(1, 128 // 4) + 1, jnp.int32)
        _lenS2 = 128 - jax.random.randint(jax.random.fold_in(_rk, 8), (64,), 0, max(1, 128 // 4) + 1, jnp.int32)
        _ctx_1024P = jax.random.normal(jax.random.fold_in(_rk, 11), (64, 16, 256), jnp.float32)
        _ctx_1024c = jax.random.dirichlet(jax.random.fold_in(_rk, 511), 0.3 * jnp.ones((16,), jnp.float32), (64, 128))
        _ctx_1024t = jnp.einsum('bsk,bkd->bsd', _ctx_1024c, _ctx_1024P)
        _ctx_1024t = _ctx_1024t * jax.lax.rsqrt(jnp.mean(jnp.square(_ctx_1024t)) + 1e-12) * 0.953939
        ctx_1024 = -1.39393e-06 + 0.999914 * (_ctx_1024t + 0.3 * jax.random.normal(jax.random.fold_in(_rk, 611), (64, 128, 256), jnp.float32))
        _g = jax.random.normal(jax.random.fold_in(_rk, 9001), (2, 1), jnp.float32)
        _g = jnp.sign(_g) * jnp.maximum(jnp.abs(_g), 1.0) + (_g == 0) * 1.0
        g_xattn = _g[0]
        g_ffn = _g[1]
        return (x, ctx_1024, g_xattn, g_ffn)
    x, ctx_1024, g_xattn, g_ffn = _rec_inputs()

    def _L0_xattn_setup():
        import jax, jax.numpy as jnp
        import numpy as np
        import math
        CHANNELS = 128
        N_HEADS = 8
        K_CH = CHANNELS // N_HEADS
        ROPE_D = int(K_CH * 0.5)
        BASE = 2500

        def _rope(x):
            d = ROPE_D
            t = x.shape[2]
            theta = 1.0 / BASE ** (jnp.arange(0, d, 2, dtype=jnp.float32) / d)
            ang = jnp.arange(t, dtype=jnp.float32)[:, None] * theta[None, :]
            ang = jnp.concatenate([ang, ang], axis=-1)
            cos = jnp.cos(ang)[None, None, :, :].astype(x.dtype)
            sin = jnp.sin(ang)[None, None, :, :].astype(x.dtype)
            x_rope, x_pass = (x[..., :d], x[..., d:])
            neg_half = jnp.concatenate([-x_rope[..., d // 2:], x_rope[..., :d // 2]], axis=-1)
            return jnp.concatenate([x_rope * cos + neg_half * sin, x_pass], axis=-1)

        def _split_heads(y):
            b, _, t = y.shape
            return y.reshape(b, N_HEADS, K_CH, t).transpose(0, 1, 3, 2)
        key = jax.random.key(seed)
        ks = jax.random.split(key, 10)
        B, T = (8, 256)
        w_scale = 1.0 / math.sqrt(CHANNELS)
        return {'x': jax.random.normal(ks[0], (B, CHANNELS, T), jnp.float32), 'c': jax.random.normal(ks[1], (B, CHANNELS, T), jnp.float32), 'Wq': jax.random.normal(ks[2], (CHANNELS, CHANNELS), jnp.float32) * w_scale, 'bq': jax.random.normal(ks[3], (CHANNELS,), jnp.float32) * 0.02, 'Wk': jax.random.normal(ks[4], (CHANNELS, CHANNELS), jnp.float32) * w_scale, 'bk': jax.random.normal(ks[5], (CHANNELS,), jnp.float32) * 0.02, 'Wv': jax.random.normal(ks[6], (CHANNELS, CHANNELS), jnp.float32) * w_scale, 'bv': jax.random.normal(ks[7], (CHANNELS,), jnp.float32) * 0.02, 'Wo': jax.random.normal(ks[8], (CHANNELS, CHANNELS), jnp.float32) * w_scale, 'bo': jax.random.normal(ks[9], (CHANNELS,), jnp.float32) * 0.02}
    _L0_xattn_all = _L0_xattn_setup()
    _L0_xattn_in = {k: v for k, v in _L0_xattn_all.items() if k in ('Wq', 'bq', 'Wk', 'bk', 'Wv', 'bv', 'Wo', 'bo')}
    del _L0_xattn_all

    def _L0_ffn_setup():
        import jax, jax.numpy as jnp
        import numpy as np
        import math
        BETA = 0.9
        THRESHOLD = 1.0
        NUM_STEPS = 5
        ALPHA = 2.0

        @jax.custom_vjp
        def spike_fn(u):
            return (u > 0).astype(u.dtype)

        def _spike_fwd(u):
            return (spike_fn(u), u)

        def _spike_bwd(u, g):
            s = jnp.pi / 2.0 * ALPHA * u
            return (g * (ALPHA / 2.0) / (1.0 + s * s),)
        spike_fn.defvjp(_spike_fwd, _spike_bwd)
        key = jax.random.key(seed)
        k1, k2, k3 = jax.random.split(key, 3)
        n_embd = 256
        x = jax.random.normal(k1, (4, 512, n_embd), dtype=jnp.float32)
        W_fc = jax.random.normal(k2, (4 * n_embd, n_embd), dtype=jnp.float32) / math.sqrt(n_embd)
        W_proj = jax.random.normal(k3, (n_embd, 4 * n_embd), dtype=jnp.float32) / math.sqrt(4 * n_embd)
        return {'x': x, 'W_fc': W_fc, 'W_proj': W_proj}
    _L0_ffn_all = _L0_ffn_setup()
    _L0_ffn_in = {k: v for k, v in _L0_ffn_all.items() if k in ('W_fc', 'W_proj')}
    del _L0_ffn_all
    return {'x': x, 'ctx_1024': ctx_1024, 'g_xattn': g_xattn, 'g_ffn': g_ffn, 'L0_xattn_Wq': _L0_xattn_in['Wq'], 'L0_xattn_bq': _L0_xattn_in['bq'], 'L0_xattn_Wk': _L0_xattn_in['Wk'], 'L0_xattn_bk': _L0_xattn_in['bk'], 'L0_xattn_Wv': _L0_xattn_in['Wv'], 'L0_xattn_bv': _L0_xattn_in['bv'], 'L0_xattn_Wo': _L0_xattn_in['Wo'], 'L0_xattn_bo': _L0_xattn_in['bo'], 'L0_ffn_W_fc': _L0_ffn_in['W_fc'], 'L0_ffn_W_proj': _L0_ffn_in['W_proj']}

def reference(x, ctx_1024, g_xattn, g_ffn, L0_xattn_Wq, L0_xattn_bq, L0_xattn_Wk, L0_xattn_bk, L0_xattn_Wv, L0_xattn_bv, L0_xattn_Wo, L0_xattn_bo, L0_ffn_W_fc, L0_ffn_W_proj):
    import jax
    import jax.numpy as jnp

    def _L0_xattn_ref(x, c, Wq, bq, Wk, bk, Wv, bv, Wo, bo):
        import jax, jax.numpy as jnp
        import numpy as np
        import math
        CHANNELS = 128
        N_HEADS = 8
        K_CH = CHANNELS // N_HEADS
        ROPE_D = int(K_CH * 0.5)
        BASE = 2500

        def _rope(x):
            d = ROPE_D
            t = x.shape[2]
            theta = 1.0 / BASE ** (jnp.arange(0, d, 2, dtype=jnp.float32) / d)
            ang = jnp.arange(t, dtype=jnp.float32)[:, None] * theta[None, :]
            ang = jnp.concatenate([ang, ang], axis=-1)
            cos = jnp.cos(ang)[None, None, :, :].astype(x.dtype)
            sin = jnp.sin(ang)[None, None, :, :].astype(x.dtype)
            x_rope, x_pass = (x[..., :d], x[..., d:])
            neg_half = jnp.concatenate([-x_rope[..., d // 2:], x_rope[..., :d // 2]], axis=-1)
            return jnp.concatenate([x_rope * cos + neg_half * sin, x_pass], axis=-1)

        def _split_heads(y):
            b, _, t = y.shape
            return y.reshape(b, N_HEADS, K_CH, t).transpose(0, 1, 3, 2)
        q = jnp.einsum('oc,bct->bot', Wq, x) + bq[None, :, None]
        k = jnp.einsum('oc,bct->bot', Wk, c) + bk[None, :, None]
        v = jnp.einsum('oc,bct->bot', Wv, c) + bv[None, :, None]
        q = _rope(_split_heads(q))
        k = _rope(_split_heads(k))
        v = _split_heads(v)
        scale = 1.0 / math.sqrt(K_CH)
        scores = jnp.einsum('bhtc,bhsc->bhts', q, k) * scale
        p_attn = jax.nn.softmax(scores, axis=-1)
        out = jnp.einsum('bhts,bhsc->bhtc', p_attn, v)
        b, _, t, _ = out.shape
        out = out.transpose(0, 1, 3, 2).reshape(b, CHANNELS, t)
        return jnp.einsum('oc,bct->bot', Wo, out) + bo[None, :, None]

    def _L0_ffn_ref(x, W_fc, W_proj):
        import jax, jax.numpy as jnp
        import numpy as np
        import math
        BETA = 0.9
        THRESHOLD = 1.0
        NUM_STEPS = 5
        ALPHA = 2.0

        @jax.custom_vjp
        def spike_fn(u):
            return (u > 0).astype(u.dtype)

        def _spike_fwd(u):
            return (spike_fn(u), u)

        def _spike_bwd(u, g):
            s = jnp.pi / 2.0 * ALPHA * u
            return (g * (ALPHA / 2.0) / (1.0 + s * s),)
        spike_fn.defvjp(_spike_fwd, _spike_bwd)
        h = jnp.square(jax.nn.relu(jnp.einsum('bsd,fd->bsf', x, W_fc)))
        y = jnp.einsum('bsf,df->bsd', h, W_proj)

        def step(mem, _):
            reset = jax.lax.stop_gradient(spike_fn(mem - THRESHOLD))
            mem_new = BETA * mem + y - reset * THRESHOLD
            spk = spike_fn(mem_new - THRESHOLD)
            return (mem_new, spk)
        mem0 = jnp.zeros_like(y)
        _, spks = jax.lax.scan(step, mem0, None, length=NUM_STEPS)
        return jnp.sum(spks, axis=0) / NUM_STEPS
    x = x + jnp.tanh(g_xattn[0]) * _L0_xattn_ref(_layernorm(x, axis=-1), ctx_1024, L0_xattn_Wq, L0_xattn_bq, L0_xattn_Wk, L0_xattn_bk, L0_xattn_Wv, L0_xattn_bv, L0_xattn_Wo, L0_xattn_bo)
    x = x + jnp.tanh(g_ffn[0]) * _L0_ffn_ref(_layernorm(x, axis=-1), L0_ffn_W_fc, L0_ffn_W_proj)
    return x

_drawn_inputs = setup_inputs


def setup_inputs(seed=0):
    import zlib

    import numpy as np

    out = dict(_drawn_inputs(seed))
    spreads = {}
    factors = {'L0_xattn_bq': 6.016, 'L0_xattn_bk': 8.0, 'L0_xattn_bv': 4.336, 'L0_xattn_bo': 3.734}
    for name, (base, spread) in spreads.items():
        noise = np.random.default_rng([zlib.crc32(name.encode()), seed]).standard_normal(out[name].shape)
        drawn = base * np.exp(spread * noise) if base else spread * noise
        out[name] = jnp.asarray(drawn.astype(out[name].dtype))
    for name, factor in factors.items():
        out[name] = (out[name] * factor).astype(out[name].dtype)
    return out
```

```python
import numpy as np
import concourse.bass as bass
from concourse import mybir
from contextlib import ExitStack

F32 = mybir.dt.float32
F32R = mybir.dt.float32r
BF16 = mybir.dt.bfloat16
ALU = mybir.AluOpType
ACT = mybir.ActivationFunctionType
AX = mybir.AxisListType

B, C, T = 64, 128, 256
H, D = 8, 16
ROT = D // 2
FF = 4 * T
NB = 2
UNITS = B // NB
W = NB * T
ITEMS = NB * H
GROUPS = ITEMS // 4
FCH = FF // 128 // 2
BETA, THRESHOLD, STEPS = 0.9, 1.0, 5
EPS = 1e-5
Q_PARTS = (0, 0, 0, 1, 1, 2)
K_PARTS = (0, 1, 2, 0, 1, 0)
KROWS = 6 * D

LEAD, LAG = 3, 2


def spike_thresholds():
    f = np.float32

    def spikes(y):
        mem, count = f(0), 0
        for _ in range(STEPS):
            reset = f(mem - f(THRESHOLD) > 0)
            mem = f(f(f(f(BETA) * mem) + y) - f(reset * f(THRESHOLD)))
            count += int(mem - f(THRESHOLD) > 0)
        return count

    found = []
    for n in range(1, STEPS + 1):
        low, high = int(f(0).view(np.uint32)), int(f(4).view(np.uint32))
        while high - low > 1:
            mid = (low + high) // 2
            if spikes(np.uint32(mid).view(f)) >= n:
                high = mid
            else:
                low = mid
        found.append(float(np.uint32(low).view(f)))
    return found


class Unit:

    def __init__(self, r, k):
        self.r, self.k = r, k
        self.par = k % 2
        self.fixed = isinstance(r, int)

    def exists(self):
        return not self.fixed or 0 <= 2 * self.r + self.k < UNITS

    def number(self):
        return 2 * self.r + self.k

    def count(self, per, plus):
        n = 2 * per * self.r + (per * self.k + plus)
        return min(n, per * UNITS) if self.fixed else n

    def pair_count(self, per, plus):
        n = per * self.r + (per * (self.k // 2) + plus)
        return n


def wait(eng, sem, value):
    if isinstance(value, int) and value <= 0:
        return
    eng.wait_ge(sem, value)


def wait_apart(eng, sem, value, met):
    if isinstance(value, int):
        wait(eng, sem, value)
        return
    value = eng.snap(value)
    eng.wait_ge(met, 16)
    eng.wait_ge(sem, value)


MAX_ITEMS = {s: [] for s in range(16)}
SC_ITEMS = {s: [] for s in range(16)}
for _n in range(ITEMS):
    MAX_ITEMS[(_n * 13) // 16].append(_n)
    SC_ITEMS[3 + (_n * 13) // 16].append(_n)
FC_SLOT = (1, 4, 7, 10)
PROJ_SLOT = (4, 7, 10, 13)
PV_SLOT = (8, 11, 14)


def build(nc, x, ctx_in, gx, gf, wq, wk, wv, wo, bq, bk, bv, bo, wfc, wproj, cos, sin, eye, out):
    thresholds = spike_thresholds()
    x_u = x.rearrange("(u b) c t -> u c b t", b=NB)
    c_u = ctx_in.rearrange("(u b) c t -> u c b t", b=NB)
    out_u = out.rearrange("(u b) c t -> u c b t", b=NB)

    ctx = ExitStack()
    with ctx:
        def sb(name, shape, dt=F32):
            return ctx.enter_context(nc.sbuf_tensor(name, shape, dt))

        def two(name, shape, dt=F32):
            return [sb(f"{name}{i}", shape, dt) for i in range(2)]

        def bank(name):
            return ctx.enter_context(nc.psum_tensor(name, [128, 512], F32))

        def sem(name):
            return ctx.enter_context(nc.semaphore(name))

        wq_sb, wk_sb, wv_sb, wo_sb = (sb(n, [C, C]) for n in ("wq_sb", "wk_sb", "wv_sb", "wo_sb"))
        eye_sb = sb("eye_sb", [128, 128])
        wfc_sb = sb("wfc_sb", [128, 2, FF])
        wfc_hi, wfc_lo = sb("wfc_hi", [128, 2, FF], F32R), sb("wfc_lo", [128, 2, FF], F32R)
        wproj_sb = sb("wproj_sb", [128, FF // 128, T])
        cos_sb, sin_sb = sb("cos_sb", [H * ROT, T]), sb("sin_sb", [H * ROT, T])
        bq_sb, bk_sb, bv_sb, bo_sb = (sb(n, [C, 1]) for n in ("bq_sb", "bk_sb", "bv_sb", "bo_sb"))
        gates = sb("gates", [128, 2])
        gate_x, gate_f = sb("gate_x", [128, 1]), sb("gate_f", [128, 1])
        bias_o = sb("bias_o", [128, 1])
        bias_t = sb("bias_t", [128, 1])
        minus_half, eps_sb = sb("minus_half", [128, NB]), sb("eps_sb", [128, NB])
        fence = sb("fence", [1, 1])

        xa, ca, xr = two("xa", [128, NB, T]), two("ca", [128, NB, T]), two("xr", [128, NB, T])
        xn, x2, fo = two("xn", [128, NB, T]), two("x2", [128, NB, T]), two("fo", [128, NB, T])
        st1, mv1, ve1, rs1 = (sb("st1", [128, NB, 6]), sb("mv1", [128, NB, 2]),
                              sb("ve1", [128, NB]), sb("rs1", [128, NB]))
        st2, mv2, ve2, rs2 = (sb("st2", [128, NB, 6]), sb("mv2", [128, NB, 2]),
                              sb("ve2", [128, NB]), sb("rs2", [128, NB]))
        qk = two("qk", [128, 2, W])
        turned = sb("turned", [H * ROT, 2, W])
        scaled = sb("scaled", [H * ROT, 2, W])
        parts = sb("parts", [128, 3, 2, W], BF16)
        qst, kst = two("qst", [128, H, W], BF16), two("kst", [128, H, W], BF16)
        vp = two("vp", [128, 2 * NB, H, 2 * D])
        mx = two("mx", [128, H, NB, 2])
        mparts = sb("mparts", [4 * H, 3, 128], BF16)
        mrest = sb("mrest", [4 * H, 128])
        probs = sb("probs", [128, 8, 2, T])
        usb = sb("usb", [128, 2, NB, T])
        oc, den, rec = sb("oc", [128, W]), sb("den", [128, W]), sb("rec", [128, W])
        on = sb("on", [128, W])
        attn = sb("attn", [128, W])
        xn2 = sb("xn2", [128, NB, T])
        xh, xl = two("xh", [128, 2, NB * C], F32R), two("xl", [128, 2, NB * C], F32R)
        relu = two("relu", [128, 2, NB * C])
        hid = sb("hid", [128, FCH, 2, NB * C])
        cnt = two("cnt", [128, W])

        score_bank = [bank("score0"), bank("score1")]
        max_bank = [bank("max0"), bank("max1")]
        u_bank, y_bank = bank("u_bank"), bank("y_bank")
        ga, gb = bank("ga"), bank("gb")

        s_w, s_small = sem("s_w"), sem("s_small")
        s_const, s_split, s_gate, s_bvo, s_bias = (sem("s_const"), sem("s_split"), sem("s_gate"),
                                                   sem("s_bvo"), sem("s_bias"))
        s_gscaled, s_half = sem("s_gscaled"), sem("s_half")
        x_in, c_in, xr_in = ([sem(f"{n}{i}") for i in range(2)] for n in ("x_in", "c_in", "xr_in"))
        st1_done, mv1_done, ve1_done, rs1_done, xn_done = (
            sem(n) for n in ("st1_done", "mv1_done", "ve1_done", "rs1_done", "xn_done"))
        st2_done, mv2_done, ve2_done, rs2_done, xn2_done = (
            sem(n) for n in ("st2_done", "mv2_done", "ve2_done", "rs2_done", "xn2_done"))
        q_mm, k_mm, v_mm = sem("q_mm"), sem("k_mm"), sem("v_mm")
        q_out, k_out, v_out = sem("q_out"), sem("k_out"), sem("v_out")
        turned_done, scaled_done, rope_done = sem("turned_done"), sem("scaled_done"), sem("rope_done")
        p1_done, r1_done, p2_done, p3_done = (sem(n) for n in ("p1_done", "r1_done", "p2_done", "p3_done"))
        stacked = [[sem(f"stacked{p}{b}") for b in range(NB)] for p in range(2)]
        max_mm, max_done, mt_mm = sem("max_mm"), sem("max_done"), sem("mt_mm")
        m1_done, mr_done, m2_done, m3_done = (sem(n) for n in ("m1_done", "mr_done", "m2_done", "m3_done"))
        m_stacked = [sem("m_stacked0"), sem("m_stacked1")]
        score_mm, exp_done, pv_mm, u_out = sem("score_mm"), sem("exp_done"), sem("pv_mm"), sem("u_out")
        u_moved = sem("u_moved")
        rec_done, on_done, wo_mm, attn_out, x2_done = (
            sem(n) for n in ("rec_done", "on_done", "wo_mm", "attn_out", "x2_done"))
        xt_mm, xh_done, xl_done = sem("xt_mm"), sem("xh_done"), sem("xl_done")
        fc_mm, relu_done, hid_done, proj_mm = (sem(n) for n in ("fc_mm", "relu_done", "hid_done", "proj_mm"))
        count_step, fo_done = sem("count_step"), sem("fo_done")
        stored = [sem("stored0"), sem("stored1")]

        def iterations(eng, body):
            def at(r, k):
                return lambda ahead: Unit(r, k + ahead)
            first, last = LAG // 2 + 1, (UNITS - LEAD) // 2 - 1
            for i in range(-LEAD, 2 * first):
                body(at(0, i))
            with eng.Fori(first, last + 1) as r:
                for k in range(2):
                    body(at(r, k))
            for i in range(2 * (last + 1), UNITS + LAG):
                body(at(0, i))

        block = ctx.enter_context(nc.Block())

        @block.sync
        def _(sp):
            for dst, src in ((wq_sb, wq), (wk_sb, wk), (wv_sb, wv), (wo_sb, wo), (eye_sb, eye)):
                sp.dma_start(dst[:, :], src).then_inc(s_w, 16)
            for dst, src in ((bq_sb, bq), (bk_sb, bk), (bv_sb, bv), (bo_sb, bo)):
                sp.dma_start(dst[:, :], src.rearrange("(c a) -> c a", a=1)).then_inc(s_small, 16)
            for n, g in enumerate((gx, gf)):
                sp.dma_start(gates[:, n:n + 1], g.rearrange("(a n) -> a n", a=1).to_broadcast([128, 1])
                             ).then_inc(s_small, 16)
            sp.dma_start(cos_sb[:, :], cos).then_inc(s_w, 16)
            sp.dma_start(sin_sb[:, :], sin).then_inc(s_w, 16)
            sp.dma_start(wfc_sb[:, :, :], wfc.rearrange("(n p) f -> p n f", p=128)).then_inc(s_w, 16)
            sp.dma_start(wproj_sb[:, :, :], wproj.rearrange("(n p) f -> p n f", p=128)).then_inc(s_w, 16)

            def stack(u, b):
                p = u.par
                wait_apart(sp, score_mm, u.count(ITEMS, (b + 1) * H - 2 * ITEMS), s_w)
                for n in range(6):
                    for dst, which, part in ((qst, 0, Q_PARTS[n]), (kst, 1, K_PARTS[n])):
                        sp.dma_start(dst[p][D * n:D * n + D, :, b * T:(b + 1) * T],
                                     parts[:, part, which, b * T:(b + 1) * T]).then_inc(stacked[p][b], 16)

            def body(at):
                u = at(3)
                if u.exists():
                    wait_apart(sp, xn_done, u.count(1, -1), s_w)
                    sp.dma_start(xa[u.par][:, :, :], x_u[u.number()]).then_inc(x_in[u.par], 16)
                u = at(0)
                if u.exists():
                    wait_apart(sp, x2_done, u.count(1, -1), s_w)
                    sp.dma_start(xr[u.par][:, :, :], x_u[u.number()]).then_inc(xr_in[u.par], 16)
                u = at(-1)
                if u.exists():
                    wait_apart(sp, u_out, u.count(2, 2), s_w)
                    wait_apart(sp, on_done, u.count(1, 0), s_w)
                    for j in range(4):
                        sp.dma_start(oc[32 * j:32 * j + 32, :],
                                     usb[32 * j:32 * j + D, :, :, :].rearrange("p g b t -> p (g b t)")
                                     ).then_inc(u_moved, 16)
                        sp.dma_start(den[32 * j:32 * j + 32, :],
                                     usb[32 * j + D:32 * j + 2 * D, :, :, :].rearrange("p g b t -> p (g b t)")
                                     ).then_inc(u_moved, 16)
                u = at(3)
                if u.exists():
                    wait_apart(sp, v_mm, u.count(1, -1), s_w)
                    sp.dma_start(ca[u.par][:, :, :], c_u[u.number()]).then_inc(c_in[u.par], 16)
                if at(2).exists():
                    wait_apart(sp, p3_done, at(2).count(1, 1), s_w)
                    stack(at(2), 0)
                u = at(1)
                if u.exists():
                    wait_apart(sp, m3_done, u.count(1, 1), s_w)
                    for n in range(3):
                        sp.dma_start(qst[u.par][KROWS + n:KROWS + n + 1, :, :].rearrange("i h t -> i (h t)"),
                                     mparts[:, n, :]).then_inc(m_stacked[u.par], 16)
                if at(2).exists():
                    stack(at(2), 1)
                u = at(-2)
                if u.exists():
                    wait_apart(sp, fo_done, u.count(1, 1), s_w)
                    sp.dma_start(out_u[u.number()], fo[u.par][:, :, :]).then_inc(stored[u.par], 16)

            iterations(sp, body)
            for p in range(2):
                sp.wait_ge(stored[p], 16 * UNITS // 2)

        @block.gpsimd
        def _(pool):
            nc.gpsimd.memset(minus_half[:, :], -0.5).then_inc(s_half, 1)
            nc.gpsimd.memset(eps_sb[:, :], EPS).then_inc(s_half, 1)
            for p in range(2):
                nc.gpsimd.memset(vp[p][:, :, :, D:2 * D], 1.0).then_inc(s_const, 1)
                pool.wait_ge(s_const, 2 * p + 1)
                nc.gpsimd.memset(kst[p][KROWS:KROWS + 3, :, :], 1.0).then_inc(s_const, 1)
                pool.wait_ge(s_const, 2 * p + 2)
            pool.wait_ge(s_half, 2)
            pool.wait_ge(s_w, 16 * 9)

            def inverse_deviation(u, mv, ve, rs, mv_done, ve_done, rs_done, used):
                wait(pool, mv_done, u.count(1, 1))
                wait(pool, used, u.count(1, 0))
                nc.gpsimd.tensor_tensor(ve[:, :], mv[:, :, 1], eps_sb[:, :], ALU.add).then_inc(ve_done, 1)
                wait(pool, ve_done, u.count(1, 1))
                nc.gpsimd.tensor_tensor(rs[:, :], ve[:, :], minus_half[:, :], ALU.pow
                                        ).then_inc(rs_done, 1)

            def square(u, f):
                n = u.count(FCH, f)
                wait(pool, relu_done, u.count(FCH, f + 1))
                wait(pool, proj_mm, u.count(FCH, f + 1 - FCH))
                nc.gpsimd.tensor_tensor(hid[:, f, :, :], relu[f % 2][:, :, :], relu[f % 2][:, :, :],
                                        ALU.mult).then_inc(hid_done, 1)

            def body(at):
                for s in range(16):
                    u = at(3)
                    if s == 5 and u.exists():
                        inverse_deviation(u, mv1, ve1, rs1, mv1_done, ve1_done, rs1_done, xn_done)
                    u = at(2)
                    if u.exists():
                        q = qk[u.par]
                        if s == 1:
                            wait(pool, q_out, u.count(1, 1))
                            wait(pool, k_out, u.count(1, 1))
                            wait(pool, rope_done, u.count(1, 0))
                            nc.gpsimd.tensor_tensor(
                                scaled[:, :, :].rearrange("p n (b t) -> p (n b) t", b=NB),
                                q[0:H * ROT, :, :].rearrange("p n (b t) -> p (n b) t", b=NB),
                                cos_sb[:, :].unsqueeze(1).to_broadcast([H * ROT, 2 * NB, T]),
                                ALU.mult).then_inc(scaled_done, 1)
                        if s == 3:
                            wait(pool, scaled_done, u.count(1, 1))
                            wait(pool, turned_done, u.count(2, 2))
                            nc.gpsimd.tensor_tensor(q[0:H * ROT, :, :], scaled[:, :, :], turned[:, :, :],
                                                    ALU.add).then_inc(rope_done, 1)
                        if s == 7:
                            wait(pool, p1_done, u.count(1, 1))
                            nc.gpsimd.tensor_tensor(q[:, :, :], q[:, :, :], parts[:, 0, :, :],
                                                    ALU.subtract).then_inc(r1_done, 1)
                        if s == 10:
                            wait(pool, p2_done, u.count(1, 1))
                            nc.gpsimd.tensor_tensor(parts[:, 2, :, :], q[:, :, :], parts[:, 1, :, :],
                                                    ALU.subtract).then_inc(p3_done, 1)
                    u = at(-1)
                    if u.exists():
                        p = u.par
                        if s == 5:
                            wait(pool, rec_done, u.count(1, 1))
                            wait(pool, wo_mm, u.count(1, 0))
                            nc.gpsimd.tensor_tensor(on[:, :], oc[:, :], rec[:, :], ALU.mult
                                                    ).then_inc(on_done, 1)
                        if s == 10:
                            wait(pool, attn_out, u.count(1, 1))
                            wait(pool, xr_in[p], u.pair_count(16, 16))
                            wait(pool, fo_done, u.count(1, -1))
                            nc.gpsimd.tensor_tensor(
                                x2[p][:, :, :], xr[p][:, :, :],
                                attn[:, :].rearrange("p (b t) -> p b t", b=NB), ALU.add
                            ).then_inc(x2_done, 1)
                        if s == 12:
                            inverse_deviation(u, mv2, ve2, rs2, mv2_done, ve2_done, rs2_done, xn2_done)
                    u = at(-2)
                    if u.exists() and s in (2, 5, 8, 11):
                        square(u, (2, 5, 8, 11).index(s))

            iterations(pool, body)

        @block.scalar
        def _(act):
            act.wait_ge(s_small, 16 * 6)
            nc.scalar.activation(gate_x[:, :], gates[:, 0:1], ACT.Tanh).then_inc(s_gate, 1)
            nc.scalar.activation(gate_f[:, :], gates[:, 1:2], ACT.Tanh).then_inc(s_gate, 1)
            act.wait_ge(s_bias, 1)

            def body(at):
                for s in range(16):
                    u = at(2)
                    if u.exists():
                        p = u.par
                        if s == 0:
                            wait(act, q_mm, u.count(1, 1))
                            wait(act, p3_done, u.count(1, -1))
                            nc.scalar.activation(qk[p][:, 0, :], ga[:, :], ACT.Identity,
                                                 bias=bq_sb[:, :]).then_inc(q_out, 1)
                            wait(act, k_mm, u.count(1, 1))
                            nc.scalar.activation(qk[p][:, 1, :], gb[:, :], ACT.Identity,
                                                 bias=bk_sb[:, :]).then_inc(k_out, 1)
                        if s == 5:
                            wait(act, rope_done, u.count(1, 1))
                            wait(act, q_out, u.count(1, 1))
                            wait(act, k_out, u.count(1, 1))
                            other = Unit(u.r, u.k - 1)
                            for b in range(NB):
                                wait(act, stacked[other.par][b], other.pair_count(192, 192))
                            nc.scalar.activation(parts[:, 0, :, :], qk[p][:, :, :], ACT.Copy
                                                 ).then_inc(p1_done, 1)
                        if s == 9:
                            wait(act, r1_done, u.count(1, 1))
                            nc.scalar.activation(parts[:, 1, :, :], qk[p][:, :, :], ACT.Copy
                                                 ).then_inc(p2_done, 1)
                    u = at(1)
                    if u.exists() and s == 2:
                        wait(act, v_mm, u.count(1, 1))
                        wait(act, pv_mm, u.count(GROUPS, -GROUPS))
                        nc.scalar.activation(
                            vp[u.par][:, :, :, 0:D], ga[:, :].rearrange("p (n h i) -> p n h i", h=H, i=D),
                            ACT.Copy).then_inc(v_out, 1)
                    u = at(-1)
                    if u.exists():
                        if s == 1:
                            copy_u(u, 1)
                        if s == 9:
                            wait(act, wo_mm, u.count(1, 1))
                            wait(act, x2_done, u.count(1, 0))
                            nc.scalar.activation(attn[:, :], ga[:, :], ACT.Identity,
                                                 scale=gate_x[:, :], bias=bias_o[:, :]).then_inc(attn_out, 1)
                        if s == 14:
                            wait(act, xt_mm, u.count(1, 1))
                            wait(act, fc_mm, u.count(FCH, -FCH))
                            nc.scalar.activation(
                                xh[u.par][:, :, :], ga[:, :].rearrange("p (n c) -> p n c", n=2), ACT.Copy
                            ).then_inc(xh_done, 1)
                    u = at(0)
                    if u.exists():
                        for n in SC_ITEMS[s]:
                            wait(act, score_mm, u.count(ITEMS, n + 1))
                            if n % 4 == 0:
                                wait(act, pv_mm, u.count(GROUPS, n // 4 - 1))
                            nc.scalar.activation(
                                probs[:, n % 8, :, :],
                                score_bank[n % 2][:, :].rearrange("p (n t) -> p n t", n=2),
                                ACT.Exp, scale=1.0 / D ** 0.5).then_inc(exp_done, 1)
                        if s == 12:
                            copy_u(u, 0)
                    u = at(-2)
                    if u.exists() and s in (2, 5, 8, 11):
                        f = (2, 5, 8, 11).index(s)
                        wait(act, fc_mm, u.count(FCH, f + 1))
                        wait(act, hid_done, u.count(FCH, f - 1))
                        nc.scalar.activation(
                            relu[f % 2][:, :, :], (gb, ga, gb, gb)[f][:, :].rearrange("p (n c) -> p n c", n=2),
                            ACT.Relu).then_inc(relu_done, 1)

            def copy_u(u, b):
                wait(act, pv_mm, u.count(GROUPS, 2 * b + 2))
                if b == 0:
                    wait(act, u_moved, u.count(128, 0))
                nc.scalar.activation(usb[:, :, b, :], u_bank[:, :].rearrange("p (g t) -> p g t", g=2),
                                     ACT.Copy).then_inc(u_out, 1)

            iterations(act, body)

        @block.vector
        def _(dve):
            dve.wait_ge(s_w, 16 * 9)
            nc.vector.tensor_copy(wfc_hi[:, :, :], wfc_sb[:, :, :]).then_inc(s_split, 1)
            dve.wait_ge(s_split, 1)
            nc.vector.tensor_tensor(wfc_lo[:, :, :], wfc_sb[:, :, :], wfc_hi[:, :, :].bitcast(F32),
                                    ALU.subtract).then_inc(s_split, 1)
            dve.wait_ge(s_bvo, 1)
            nc.vector.tensor_tensor(bias_t[:, :], ga[:, 0:1], bo_sb[:, :], ALU.add).then_inc(s_gscaled, 1)
            dve.wait_ge(s_gate, 2)
            dve.wait_ge(s_gscaled, 1)
            nc.vector.tensor_tensor(bias_o[:, :], bias_t[:, :], gate_x[:, :], ALU.mult).then_inc(s_bias, 1)
            nc.vector.tensor_scalar(gates[:, 1:2], gate_f[:, :], 1.0 / STEPS, None, ALU.mult
                                    ).then_inc(s_gscaled, 1)
            dve.wait_ge(s_gscaled, 2)

            def statistics(u, src, st, mv, st_done, mv_done, norm_done):
                for b in range(NB):
                    last = nc.vector.bn_stats(st[:, b, :], src[:, b, :])
                last.then_inc(st_done, 1)
                wait(dve, st_done, u.count(1, 1))
                nc.vector.memset(fence[:, :], 0.0)
                for b in range(NB):
                    last = nc.vector.bn_aggr(mv[:, b, :], st[:, b, :])
                last.then_inc(mv_done, 1)

            def normalize(u, dst, src, mv, rs, rs_done, done):
                wait(dve, rs_done, u.count(1, 1))
                for b in range(NB):
                    last = nc.vector.tensor_scalar(dst[:, b, :], src[:, b, :], mv[:, b, 0:1],
                                                   rs[:, b:b + 1], ALU.subtract, ALU.mult)
                last.then_inc(done, 1)

            def body(at):
                for s in range(16):
                    u = at(3)
                    if u.exists():
                        p = u.par
                        if s == 4:
                            wait(dve, x_in[p], u.pair_count(16, 16))
                            wait(dve, xn_done, u.count(1, 0))
                            statistics(u, xa[p], st1, mv1, st1_done, mv1_done, xn_done)
                        if s == 7:
                            wait(dve, q_mm, u.count(1, -1))
                            normalize(u, xn[p], xa[p], mv1, rs1, rs1_done, xn_done)
                    u = at(2)
                    if u.exists() and s == 2:
                        q = qk[u.par]
                        wait(dve, q_out, u.count(1, 1))
                        wait(dve, k_out, u.count(1, 1))
                        wait(dve, rope_done, u.count(1, 0))
                        half = H * ROT // 2
                        for src, dst in ((half, 0), (0, half)):
                            nc.vector.tensor_tensor(
                                turned[dst:dst + half, :, :].rearrange("p n (b t) -> p (n b) t", b=NB),
                                q[src:src + half, :, :].rearrange("p n (b t) -> p (n b) t", b=NB),
                                sin_sb[src:src + half, :].unsqueeze(1).to_broadcast([half, 2 * NB, T]),
                                ALU.mult).then_inc(turned_done, 1)
                    u = at(-1)
                    if u.exists():
                        if s == 5:
                            wait(dve, u_moved, u.count(128, 128))
                            wait(dve, on_done, u.count(1, 0))
                            nc.vector.reciprocal(rec[:, :], den[:, :]).then_inc(rec_done, 1)
                        if s == 11:
                            wait(dve, x2_done, u.count(1, 1))
                            wait(dve, xn2_done, u.count(1, 0))
                            statistics(u, x2[u.par], st2, mv2, st2_done, mv2_done, xn2_done)
                        if s == 12:
                            wait(dve, xt_mm, u.count(1, 0))
                            normalize(u, xn2, x2[u.par], mv2, rs2, rs2_done, xn2_done)
                        if s == 14:
                            wait(dve, xh_done, u.count(1, 1))
                            nc.vector.tensor_tensor(
                                xl[u.par][:, :, :], ga[:, :].rearrange("p (n c) -> p n c", n=2),
                                xh[u.par][:, :, :].bitcast(F32), ALU.subtract).then_inc(xl_done, 1)
                    u = at(1)
                    if u.exists():
                        for n in MAX_ITEMS[s]:
                            b, h = n // H, n % H
                            if n == 0:
                                wait(dve, mt_mm, u.count(1, -1))
                            wait(dve, max_mm, u.count(ITEMS, n + 1))
                            nc.vector.tensor_reduce(
                                mx[u.par][:, h, b, :], max_bank[n % 2][:, :].rearrange("p (n t) -> p n t", n=2),
                                AX.X, ALU.max, negate=True).then_inc(max_done, 1)
                        if s == 13:
                            wait(dve, mt_mm, u.count(1, 1))
                            other = Unit(u.r, u.k - 1)
                            wait(dve, m_stacked[other.par], other.pair_count(48, 48))
                            m = gb[0:4 * H, 0:128]
                            nc.vector.tensor_copy(mparts[:, 0, :], m).then_inc(m1_done, 1)
                            wait(dve, m1_done, u.count(1, 1))
                            nc.vector.tensor_tensor(mrest[:, :], m, mparts[:, 0, :], ALU.subtract
                                                    ).then_inc(mr_done, 1)
                            wait(dve, mr_done, u.count(1, 1))
                            nc.vector.tensor_copy(mparts[:, 1, :], mrest[:, :]).then_inc(m2_done, 1)
                            wait(dve, m2_done, u.count(1, 1))
                            nc.vector.tensor_tensor(mparts[:, 2, :], mrest[:, :], mparts[:, 1, :],
                                                    ALU.subtract).then_inc(m3_done, 1)
                    u = at(-2)
                    if u.exists() and s == 15:
                        wait(dve, proj_mm, u.count(FCH, FCH))
                        wait(dve, fo_done, u.count(1, 0))
                        y = y_bank[:, :]
                        nc.vector.tensor_scalar(cnt[0][:, :], y, thresholds[0], None, ALU.is_gt
                                                ).then_inc(count_step, 1)
                        for n in range(1, STEPS):
                            wait(dve, count_step, u.count(STEPS, n))
                            nc.vector.scalar_tensor_tensor(
                                out=cnt[n % 2][:, :], in0=y, scalar=thresholds[n],
                                in1=cnt[(n - 1) % 2][:, :], op0=ALU.is_gt, op1=ALU.add
                            ).then_inc(count_step, 1)
                        wait(dve, count_step, u.count(STEPS, STEPS))
                        wait(dve, stored[u.par], u.pair_count(16, 0))
                        nc.vector.scalar_tensor_tensor(
                            out=fo[u.par][:, :, :],
                            in0=cnt[(STEPS - 1) % 2][:, :].rearrange("p (b t) -> p b t", b=NB),
                            scalar=gates[:, 1:2], in1=x2[u.par][:, :, :], op0=ALU.mult, op1=ALU.add
                        ).then_inc(fo_done, 1)

            iterations(dve, body)

        @block.tensor
        def _(pe):
            pe.wait_ge(s_w, 16 * 9)
            pe.wait_ge(s_small, 16 * 6)
            nc.tensor.matmul(ga[:, 0:1], wo_sb[:, :], bv_sb[:, :], start=True, stop=True).then_inc(s_bvo, 1)
            pe.wait_ge(s_bias, 1)
            pe.wait_ge(s_const, 4)
            pe.wait_ge(s_split, 2)

            def project_qk(u):
                p = u.par
                wait(pe, xn_done, u.count(1, 1))
                wait(pe, xl_done, u.count(1, -3))
                wait(pe, v_out, u.count(1, -1))
                nc.tensor.matmul(ga[:, :], wq_sb[:, :], xn[p][:, :, :].rearrange("c b t -> c (b t)"),
                                 start=True, stop=True).then_inc(q_mm, 1)
                wait(pe, c_in[p], u.pair_count(16, 16))
                wait(pe, mr_done, u.count(1, -1))
                wait(pe, k_out, u.count(1, 0))
                nc.tensor.matmul(gb[:, :], wk_sb[:, :], ca[p][:, :, :].rearrange("c b t -> c (b t)"),
                                 start=True, stop=True).then_inc(k_mm, 1)

            def project_v(u):
                p = u.par
                wait(pe, q_out, Unit(u.r, u.k + 1).count(1, 1))
                wait(pe, c_in[p], u.pair_count(16, 16))
                for n in range(2 * NB):
                    last = nc.tensor.matmul(ga[:, n * C:(n + 1) * C],
                                            ca[p][:, n // 2, (n % 2) * 128:(n % 2) * 128 + 128],
                                            wv_sb[:, :], start=True, stop=True)
                last.then_inc(v_mm, 1)

            def max_item(u, n):
                b, h = n // H, n % H
                q, k = qst[u.par], kst[u.par]
                if h == 0:
                    wait(pe, stacked[u.par][b], u.pair_count(192, 192))
                wait(pe, max_done, u.count(ITEMS, n - 1))
                for half in range(2):
                    t0 = b * T + half * 128
                    last = nc.tensor.matmul(max_bank[n % 2][:, half * T:(half + 1) * T],
                                            q[0:KROWS, h, t0:t0 + 128], k[0:KROWS, h, b * T:(b + 1) * T],
                                            start=True, stop=True)
                last.then_inc(max_mm, 1)

            def score_item(u, n):
                b, h = n // H, n % H
                q, k = qst[u.par], kst[u.par]
                if n == 0:
                    wait(pe, m_stacked[u.par], u.pair_count(48, 48))
                wait(pe, exp_done, u.count(ITEMS, n - 1))
                for half in range(2):
                    s0 = b * T + half * 128
                    last = nc.tensor.matmul(score_bank[n % 2][:, half * T:(half + 1) * T],
                                            k[0:KROWS + 3, h, s0:s0 + 128],
                                            q[0:KROWS + 3, h, b * T:(b + 1) * T], start=True, stop=True)
                last.then_inc(score_mm, 1)

            def v_products(u, g):
                b, top = g // 2, g % 2
                wait(pe, exp_done, u.count(ITEMS, 4 * g + 4))
                if g == 0:
                    wait(pe, v_out, u.count(1, 1))
                if top == 0:
                    wait(pe, u_out, u.count(2, b))
                for half in range(2):
                    for j in range(4):
                        last = nc.tensor.matmul(
                            u_bank[32 * j:32 * j + 32, top * T:(top + 1) * T],
                            vp[u.par][:, 2 * b + half, 4 * top + j, :],
                            probs[:, (4 * g + j) % 8, half, :], start=(half == 0), stop=(half == 1))
                last.then_inc(pv_mm, 1)

            def first_product(u, f):
                p = u.par
                if f == 0:
                    wait(pe, xl_done, u.count(1, 1))
                    wait(pe, k_out, Unit(u.r, u.k + 4).count(1, 1))
                elif f == 1:
                    wait(pe, v_out, Unit(u.r, u.k + 3).count(1, 1))
                else:
                    wait(pe, relu_done, u.count(FCH, (1, 3)[f - 2]))
                dst = (gb, ga, gb, gb)[f]
                for half in range(2):
                    f0 = (2 * f + half) * 128
                    n = 0
                    for dc in range(2):
                        for w, xx in ((wfc_hi, xh), (wfc_hi, xl), (wfc_lo, xh)):
                            last = nc.tensor.matmul(dst[:, half * 256:half * 256 + 256],
                                                    w[:, dc, f0:f0 + 128], xx[p][:, dc, :],
                                                    start=(n == 0), stop=(n == 5))
                            n += 1
                last.then_inc(fc_mm, 1)

            def second_product(u, f):
                wait(pe, hid_done, u.count(FCH, f + 1))
                if f == 0:
                    wait(pe, count_step, u.count(STEPS, 0))
                for half in range(2):
                    for b in range(NB):
                        last = nc.tensor.matmul(
                            y_bank[:, b * T:(b + 1) * T], hid[:, f, half, b * C:(b + 1) * C],
                            wproj_sb[:, 2 * f + half, :], start=(f == 0 and half == 0 and b == 0),
                            stop=(f == FCH - 1 and half == 1), skip_group_check=True)
                last.then_inc(proj_mm, 1)

            def body(at):
                for s in range(16):
                    if s == 0 and at(2).exists():
                        project_qk(at(2))
                    if s == 2 and at(1).exists():
                        project_v(at(1))
                    if s == 1 and at(-1).exists():
                        v_products(at(-1), 3)
                    if at(1).exists():
                        for n in MAX_ITEMS[s]:
                            max_item(at(1), n)
                    if at(0).exists():
                        for n in SC_ITEMS[s]:
                            score_item(at(0), n)
                        if s in PV_SLOT:
                            v_products(at(0), PV_SLOT.index(s))
                    u = at(-2)
                    if u.exists():
                        if s in PROJ_SLOT and s != FC_SLOT[0]:
                            second_product(u, PROJ_SLOT.index(s))
                        if s in FC_SLOT:
                            first_product(u, FC_SLOT.index(s))
                    u = at(-1)
                    if u.exists():
                        if s == 8:
                            wait(pe, on_done, u.count(1, 1))
                            wait(pe, relu_done, Unit(u.r, u.k - 1).count(FCH, 2))
                            wait(pe, v_out, Unit(u.r, u.k + 2).count(1, 1))
                            nc.tensor.matmul(ga[:, :], wo_sb[:, :], on[:, :], start=True, stop=True
                                             ).then_inc(wo_mm, 1)
                        if s == 13:
                            wait(pe, xn2_done, u.count(1, 1))
                            for dc in range(2):
                                for b in range(NB):
                                    o = (dc * NB + b) * 128
                                    last = nc.tensor.transpose(ga[:, o:o + 128],
                                                               xn2[:, b, dc * 128:(dc + 1) * 128],
                                                               eye_sb[:, :])
                            last.then_inc(xt_mm, 1)
                    if s == 13 and at(1).exists():
                        u = at(1)
                        wait(pe, max_done, u.count(ITEMS, ITEMS))
                        wait(pe, relu_done, Unit(u.r, u.k - 3).count(FCH, FCH))
                        wait(pe, k_out, Unit(u.r, u.k + 1).count(1, 1))
                        nc.tensor.transpose(gb[0:4 * H, 0:128],
                                            mx[u.par][:, :, :, :].rearrange("p h b n -> p (h b n)"),
                                            eye_sb[:, :]).then_inc(mt_mm, 1)

            iterations(pe, body)


_NAMES = ("x", "ctx", "gx", "gf", "wq", "wk", "wv", "wo", "bq", "bk", "bv", "bo", "wfc", "wproj",
          "cos", "sin", "eye")


def kernel(x, ctx_1024, g_xattn, g_ffn, L0_xattn_Wq, L0_xattn_bq, L0_xattn_Wk, L0_xattn_bk,
           L0_xattn_Wv, L0_xattn_bv, L0_xattn_Wo, L0_xattn_bo, L0_ffn_W_fc, L0_ffn_W_proj):
    import concourse.bacc as bacc
    from concourse.bass_utils import run_bass_kernel_spmd as run

    order = np.arange(C).reshape(H, D).T.reshape(-1)
    out_order = np.arange(C).reshape(2, 4, D).transpose(1, 2, 0).reshape(-1)
    wq, wk, wv, wo = (np.asarray(w) for w in (L0_xattn_Wq, L0_xattn_Wk, L0_xattn_Wv, L0_xattn_Wo))

    theta = (1.0 / np.float32(2500) ** (np.arange(0, ROT, 2, dtype=np.float32) / np.float32(ROT))
             ).astype(np.float32)
    angle = np.arange(T, dtype=np.float32)[None, :] * theta[:, None]
    cos = np.repeat(np.cos(angle), H, axis=0)
    sin = np.repeat(np.sin(angle), H, axis=0)
    arrays = {
        "x": np.asarray(x), "ctx": np.asarray(ctx_1024), "gx": np.asarray(g_xattn), "gf": np.asarray(g_ffn),
        "wq": wq[order].T, "wk": wk[order].T, "wv": wv.T, "wo": wo.T[out_order],
        "bq": np.asarray(L0_xattn_bq)[order], "bk": np.asarray(L0_xattn_bk)[order],
        "bv": np.asarray(L0_xattn_bv)[out_order], "bo": np.asarray(L0_xattn_bo),
        "wfc": np.asarray(L0_ffn_W_fc).T, "wproj": np.asarray(L0_ffn_W_proj).T,
        "cos": np.concatenate([cos, cos]), "sin": np.concatenate([sin, -sin]),
        "eye": np.eye(128, dtype=np.float32),
    }
    arrays = {f"in_{n}": np.ascontiguousarray(arrays[n], dtype=np.float32) for n in _NAMES}
    nc = bacc.Bacc("TRN2", target_bir_lowering=False, num_devices=1)
    args = [nc.dram_tensor(n, a.shape, F32, kind="ExternalInput").ap() for n, a in arrays.items()]
    out = nc.dram_tensor("out_0", (B, C, T), F32, kind="ExternalOutput").ap()
    build(nc, *args, out)
    r = run(nc, [arrays], core_ids=[0])
    return r.results[0]["out_0"]
```

```python
import numpy as np
import concourse.bass as bass
from concourse import mybir
from contextlib import ExitStack

F32 = mybir.dt.float32
F32R = mybir.dt.float32r
BF16 = mybir.dt.bfloat16
ALU = mybir.AluOpType
ACT = mybir.ActivationFunctionType
AX = mybir.AxisListType

B, C, T = 64, 128, 256
H, D = 8, 16
ROT = D // 2
FF = 4 * T
NB = 2
UNITS = B // NB
W = NB * T
ITEMS = NB * H
GROUPS = ITEMS // 4
FCH = FF // 128 // 2
BETA, THRESHOLD, STEPS = 0.9, 1.0, 5
EPS = 1e-5
Q_PARTS = (0, 0, 0, 1, 1, 2)
K_PARTS = (0, 1, 2, 0, 1, 0)
KROWS = 6 * D

LEAD, LAG = 3, 3


def spike_thresholds():
    f = np.float32

    def spikes(y):
        mem, count = f(0), 0
        for _ in range(STEPS):
            reset = f(mem - f(THRESHOLD) > 0)
            mem = f(f(f(f(BETA) * mem) + y) - f(reset * f(THRESHOLD)))
            count += int(mem - f(THRESHOLD) > 0)
        return count

    found = []
    for n in range(1, STEPS + 1):
        low, high = int(f(0).view(np.uint32)), int(f(4).view(np.uint32))
        while high - low > 1:
            mid = (low + high) // 2
            if spikes(np.uint32(mid).view(f)) >= n:
                high = mid
            else:
                low = mid
        found.append(float(np.uint32(low).view(f)))
    return found


class Unit:

    def __init__(self, r, k):
        self.r, self.k = r, k
        self.par = k % 2
        self.fixed = isinstance(r, int)

    def exists(self):
        return not self.fixed or 0 <= 2 * self.r + self.k < UNITS

    def number(self):
        return 2 * self.r + self.k

    def count(self, per, plus):
        n = 2 * per * self.r + (per * self.k + plus)
        return min(n, per * UNITS) if self.fixed else n

    def pair_count(self, per, plus):
        n = per * self.r + (per * (self.k // 2) + plus)
        return n


def wait(eng, sem, value):
    if isinstance(value, int) and value <= 0:
        return
    eng.wait_ge(sem, value)


def wait_apart(eng, sem, value, met):
    if isinstance(value, int):
        wait(eng, sem, value)
        return
    value = eng.snap(value)
    eng.wait_ge(met, 16)
    eng.wait_ge(sem, value)


SLOTS = 32
SCHEDULE = {
    "q": [0], "k": [0], "v": [2], "max": [1, 1, 3, 4, 6, 8, 9, 11, 13, 14, 16, 17, 19, 21, 22, 24],
    "turn_max": [26], "score": [4, 7, 9, 11, 13, 14, 15, 17, 19, 20, 22, 23, 25, 27, 28, 30],
    "v_product": [16, 22, 28, 34], "wo": [27], "turn": [10], "fc": [15, 17, 20, 22],
    "proj": [25, 25, 29, 33, 33, 35, 36, 40],
    "q_out": [0], "k_out": [0], "part1": [12], "part2": [13], "v_out": [6],
    "exp": [8, 9, 11, 12, 12, 14, 15, 17, 19, 20, 22, 23, 25, 27, 28, 30], "u_out": [22, 34],
    "attn": [27], "xh": [12], "relu": [16, 18, 22, 24], "square": [18, 20, 23, 27],
    "high": [20, 22, 26, 28], "y_out": [10],
    "rs1": [18], "scaled": [2], "rope": [8], "rest1": [8], "part3": [18], "gated": [21], "x2": [28],
    "rs2": [6], "low": [20, 24, 27, 29],
    "stats1": [16], "norm1": [23], "turned": [1, 2],
    "take_max": [0, 1, 3, 4, 6, 8, 9, 11, 13, 14, 16, 17, 19, 21, 23, 27], "max_parts": [30],
    "recip": [10], "stats2": [2], "norm2": [6], "xl": [11], "count": [12, 14, 14, 18, 20, 22],
    "load_x": [0], "load_ctx": [4], "load_residual": [1], "stack": [24, 30], "stack_max": [28],
    "move_sums": [2], "move_v": [3], "put_sums": [10], "spread_sums": [11], "store": [22],
}


def due(at, s, ahead, step, n=0):
    slot = SCHEDULE[step][n]
    u = at(ahead - slot // SLOTS)
    return u if slot % SLOTS == s and u.exists() else None


def build(nc, x, ctx_in, gx, gf, wq, wk, wv, wo, bq, bk, bv, bo, wfc, wproj, cos, sin, eye, out,
          scratch):
    thresholds = spike_thresholds()
    x_u = x.rearrange("(u b) c t -> u c b t", b=NB)
    c_u = ctx_in.rearrange("(u b) c t -> u c b t", b=NB)
    out_u = out.rearrange("(u b) c t -> u c b t", b=NB)

    ctx = ExitStack()
    with ctx:
        def sb(name, shape, dt=F32):
            return ctx.enter_context(nc.sbuf_tensor(name, shape, dt))

        def two(name, shape, dt=F32):
            return [sb(f"{name}{i}", shape, dt) for i in range(2)]

        def bank(name):
            return ctx.enter_context(nc.psum_tensor(name, [128, 512], F32))

        def sem(name):
            return ctx.enter_context(nc.semaphore(name))

        wq_sb, wk_sb, wv_sb, wo_sb = (sb(n, [C, C]) for n in ("wq_sb", "wk_sb", "wv_sb", "wo_sb"))
        eye_sb = sb("eye_sb", [128, 128])
        wfc_hi, wfc_lo = sb("wfc_hi", [128, 2, FF], F32R), sb("wfc_lo", [128, 2, FF], F32R)
        wproj_hi, wproj_lo = (sb(n, [128, FF // 128, T], F32R) for n in ("wproj_hi", "wproj_lo"))
        wproj_sb = sb("wproj_sb", [128, FF // 128, T])
        cos_sb, sin_sb = sb("cos_sb", [H * ROT, T]), sb("sin_sb", [H * ROT, T])
        bq_sb, bk_sb, bv_sb, bo_sb = (sb(n, [C, 1]) for n in ("bq_sb", "bk_sb", "bv_sb", "bo_sb"))
        gates = sb("gates", [128, 2])
        gate_x, gate_f = sb("gate_x", [128, 1]), sb("gate_f", [128, 1])
        bias_o = sb("bias_o", [128, 1])
        bias_t = sb("bias_t", [128, 1])
        minus_half, eps_sb = sb("minus_half", [128, NB]), sb("eps_sb", [128, NB])
        fence = sb("fence", [1, 1])

        xa, ca, xr = two("xa", [128, NB, T]), two("ca", [128, NB, T]), two("xr", [128, NB, T])
        xn, x2, fo = two("xn", [128, NB, T]), two("x2", [128, NB, T]), two("fo", [128, NB, T])
        st1, mv1, ve1, rs1 = (sb("st1", [128, NB, 6]), sb("mv1", [128, NB, 2]),
                              sb("ve1", [128, NB]), sb("rs1", [128, NB]))
        st2, mv2, ve2, rs2 = (sb("st2", [128, NB, 6]), sb("mv2", [128, NB, 2]),
                              sb("ve2", [128, NB]), sb("rs2", [128, NB]))
        qk = two("qk", [128, 2, W])
        turned = sb("turned", [H * ROT, 2, W])
        scaled = sb("scaled", [H * ROT, 2, W])
        parts = sb("parts", [128, 6, W], BF16)
        stack = two("stack", [128, NB, H, 2, T], BF16)
        vp = two("vp", [128, 2 * NB, H, 2 * D])
        mx = two("mx", [128, 2, NB, H])
        mparts = sb("mparts", [ITEMS, 3, T], BF16)
        mrest = sb("mrest", [ITEMS, T])
        probs = sb("probs", [128, 8, 2, T])
        wfc_sb = probs[:, 0:4, :, :].rearrange("p a n t -> p (a n t)").rearrange("p (n f) -> p n f", n=2)
        usb = sb("usb", [128, 2, NB, T])
        oc, rec = sb("oc", [128, W]), sb("rec", [128, W])
        sums, rsums = sb("sums", [128, 8 * W // 128]), sb("rsums", [128, 8 * W // 128])
        on = sb("on", [128, W])
        attn = sb("attn", [128, W])
        xn2 = sb("xn2", [128, NB, T])
        xh, xl = two("xh", [128, 2, NB * C], F32R), two("xl", [128, 2, NB * C], F32R)
        relu = two("relu", [128, 2, NB * C])
        hid = two("hid", [128, 2, NB * C])
        hid_hi, hid_lo = (sb(n, [128, FCH, 2, NB * C], F32R) for n in ("hid_hi", "hid_lo"))
        y_sb = sb("y_sb", [128, W])
        cnt = two("cnt", [128, W])

        score_bank = [bank("score0"), bank("score1")]
        max_bank = [bank("max0"), bank("max1")]
        u_bank, y_bank = bank("u_bank"), bank("y_bank")
        ga, gb = bank("ga"), bank("gb")

        s_wqk, s_w, s_small, s_ffn = sem("s_wqk"), sem("s_w"), sem("s_small"), sem("s_ffn")
        s_const, s_split, s_gate, s_bvo, s_bias = (sem("s_const"), sem("s_split"), sem("s_gate"),
                                                   sem("s_bvo"), sem("s_bias"))
        s_gscaled, s_half = sem("s_gscaled"), sem("s_half")
        x_in, c_in, xr_in = ([sem(f"{n}{i}") for i in range(2)] for n in ("x_in", "c_in", "xr_in"))
        st1_done, mv1_done, ve1_done, rs1_done, xn_done = (
            sem(n) for n in ("st1_done", "mv1_done", "ve1_done", "rs1_done", "xn_done"))
        st2_done, mv2_done, ve2_done, rs2_done, xn2_done = (
            sem(n) for n in ("st2_done", "mv2_done", "ve2_done", "rs2_done", "xn2_done"))
        q_mm, k_mm, v_mm = sem("q_mm"), sem("k_mm"), sem("v_mm")
        q_out, k_out, v_out = sem("q_out"), sem("k_out"), sem("v_out")
        turned_done, scaled_done, rope_done = sem("turned_done"), sem("scaled_done"), sem("rope_done")
        p1_done, r1_done, p2_done, p3_done = (sem(n) for n in ("p1_done", "r1_done", "p2_done", "p3_done"))
        stacked = [[sem(f"stacked{p}{b}") for b in range(NB)] for p in range(2)]
        max_mm, max_done, mt_mm = sem("max_mm"), sem("max_done"), sem("mt_mm")
        m1_done, mr_done, m2_done, m3_done = (sem(n) for n in ("m1_done", "mr_done", "m2_done", "m3_done"))
        m_stacked = [sem("m_stacked0"), sem("m_stacked1")]
        score_mm, exp_done, pv_mm, u_out = sem("score_mm"), sem("exp_done"), sem("pv_mm"), sem("u_out")
        oc_in = sem("oc_in")
        sums_in, rsums_done, rsums_out, rec_in = (
            sem(n) for n in ("sums_in", "rsums_done", "rsums_out", "rec_in"))
        on_done, wo_mm, attn_out, x2_done = (
            sem(n) for n in ("on_done", "wo_mm", "attn_out", "x2_done"))
        xt_mm, xh_done, xl_done = sem("xt_mm"), sem("xh_done"), sem("xl_done")
        fc_mm, relu_done, hid_done, hi_done, lo_done, proj_mm, y_out = (
            sem(n) for n in ("fc_mm", "relu_done", "hid_done", "hi_done", "lo_done", "proj_mm", "y_out"))
        count_step, fo_done = sem("count_step"), sem("fo_done")
        stored = [sem("stored0"), sem("stored1")]

        def iterations(eng, body, once=lambda i: None):
            def at(r, k):
                return lambda ahead: Unit(r, k + ahead)
            first, last = LAG // 2 + 2, (UNITS - LEAD) // 2 - 1
            for i in range(-LEAD, 2 * first):
                body(at(0, i))
                once(i)
            with eng.Fori(first, last + 1) as r:
                for k in range(2):
                    body(at(r, k))
            for i in range(2 * (last + 1), UNITS + LAG):
                body(at(0, i))

        block = ctx.enter_context(nc.Block())

        @block.sync
        def _(sp):
            def once(i):
                if i == -LEAD:
                    for dst, src in ((wq_sb, wq), (wk_sb, wk)):
                        sp.dma_start(dst[:, :], src).then_inc(s_wqk, 16)
                    for dst, src in ((bq_sb, bq), (bk_sb, bk), (bv_sb, bv), (bo_sb, bo)):
                        sp.dma_start(dst[:, :], src.rearrange("(c a) -> c a", a=1)).then_inc(s_small, 16)
                    for n, g in enumerate((gx, gf)):
                        sp.dma_start(gates[:, n:n + 1],
                                     g.rearrange("(a n) -> a n", a=1).to_broadcast([128, 1])
                                     ).then_inc(s_small, 16)
                    for dst, src in ((cos_sb, cos), (sin_sb, sin), (wv_sb, wv), (wo_sb, wo), (eye_sb, eye)):
                        sp.dma_start(dst[:, :], src).then_inc(s_w, 16)
                    sp.dma_start(wfc_sb[:, :, :], wfc.rearrange("(n p) f -> p n f", p=128)).then_inc(s_ffn, 16)
                    sp.dma_start(wproj_sb[:, :, :], wproj.rearrange("(n p) f -> p n f", p=128)).then_inc(s_ffn, 16)

            def stack_parts(u, b):
                wait_apart(sp, p3_done, u.count(1, 1), s_w)
                wait_apart(sp, score_mm, u.count(ITEMS, (b + 1) * H - 2 * ITEMS), s_w)
                cols = slice(b * T, (b + 1) * T)
                for n, (qp, kp) in enumerate(zip(Q_PARTS, K_PARTS)):
                    sp.dma_start(stack[u.par][D * n:D * n + D, b, :, :, :],
                                 parts[:, qp:kp + 4:3 + kp - qp, cols]).then_inc(stacked[u.par][b], 16)

            def body(at):
                for s in range(SLOTS):
                    if u := due(at, s, 3, "load_x"):
                        wait_apart(sp, xn_done, u.count(1, -1), s_w)
                        sp.dma_start(xa[u.par][:, :, :], x_u[u.number()]).then_inc(x_in[u.par], 16)
                    if u := due(at, s, 3, "load_ctx"):
                        wait_apart(sp, v_mm, u.count(1, -1), s_w)
                        sp.dma_start(ca[u.par][:, :, :], c_u[u.number()]).then_inc(c_in[u.par], 16)
                    if u := due(at, s, 0, "load_residual"):
                        wait_apart(sp, x2_done, u.count(1, -1), s_w)
                        sp.dma_start(xr[u.par][:, :, :], x_u[u.number()]).then_inc(xr_in[u.par], 16)
                    if u := due(at, s, -1, "move_sums"):
                        wait_apart(sp, u_out, u.count(2, 2), s_w)
                        for j in range(4):
                            sp.dma_start(sums[32 * j:32 * j + 32, :],
                                         usb[32 * j + D:32 * j + D + 1, :, :, :].rearrange("p g b t -> p (g b t)")
                                         ).then_inc(sums_in, 16)
                    if u := due(at, s, -1, "move_v"):
                        wait_apart(sp, u_out, u.count(2, 2), s_w)
                        wait_apart(sp, on_done, u.count(1, 0), s_w)
                        for j in range(4):
                            sp.dma_start(oc[32 * j:32 * j + 32, :],
                                         usb[32 * j:32 * j + D, :, :, :].rearrange("p g b t -> p (g b t)")
                                         ).then_inc(oc_in, 16)
                    if u := due(at, s, -1, "put_sums"):
                        wait_apart(sp, rsums_done, u.count(1, 1), s_w)
                        wait_apart(sp, rec_in, u.count(64, 0), s_w)
                        sp.dma_start(scratch.rearrange("j g n -> (j g n)").rearrange("(p n) -> p n", p=128),
                                     rsums[:, :]).then_inc(rsums_out, 16)
                    if u := due(at, s, -1, "spread_sums"):
                        wait_apart(sp, rsums_out, u.count(16, 16), s_w)
                        wait_apart(sp, on_done, u.count(1, 0), s_w)
                        for j in range(4):
                            sp.dma_start(rec[32 * j:32 * j + 32, :],
                                         scratch[j].unsqueeze(0).to_broadcast([D, 2, W])).then_inc(rec_in, 16)
                    if u := due(at, s, -3, "store"):
                        wait_apart(sp, fo_done, u.count(1, 1), s_w)
                        sp.dma_start(out_u[u.number()], fo[u.par][:, :, :]).then_inc(stored[u.par], 16)
                    for b in range(NB):
                        if u := due(at, s, 2, "stack", b):
                            stack_parts(u, b)
                    if u := due(at, s, 1, "stack_max"):
                        wait_apart(sp, m3_done, u.count(1, 1), s_w)
                        for n in range(3):
                            sp.dma_start(stack[u.par][KROWS + n:KROWS + n + 1, :, :, 0, :],
                                         mparts[:, n, :]).then_inc(m_stacked[u.par], 16)

            iterations(sp, body, once)
            for p in range(2):
                sp.wait_ge(stored[p], 16 * UNITS // 2)

        @block.gpsimd
        def _(pool):
            nc.gpsimd.memset(minus_half[:, :], -0.5).then_inc(s_half, 1)
            nc.gpsimd.memset(eps_sb[:, :], EPS).then_inc(s_half, 1)
            pool.wait_ge(s_half, 2)

            def once(i):
                if i == -LEAD:
                    for p in range(2):
                        nc.gpsimd.memset(vp[p][:, :, :, D:2 * D], 1.0).then_inc(s_const, 1)
                    pool.wait_ge(s_w, 16 * 5)

            def inverse_deviation(u, mv, ve, rs, mv_done, ve_done, rs_done, used):
                wait(pool, mv_done, u.count(1, 1))
                wait(pool, used, u.count(1, 0))
                nc.gpsimd.tensor_tensor(ve[:, :], mv[:, :, 1], eps_sb[:, :], ALU.add).then_inc(ve_done, 1)
                wait(pool, ve_done, u.count(1, 1))
                nc.gpsimd.tensor_tensor(rs[:, :], ve[:, :], minus_half[:, :], ALU.pow
                                        ).then_inc(rs_done, 1)

            def low_half(u, f):
                wait(pool, hi_done, u.count(FCH, f + 1))
                wait(pool, proj_mm, u.count(FCH, f + 1 - FCH))
                nc.gpsimd.tensor_tensor(hid_lo[:, f, :, :], hid[f % 2][:, :, :],
                                        hid_hi[:, f, :, :].bitcast(F32), ALU.subtract).then_inc(lo_done, 1)

            def body(at):
                for s in range(SLOTS):
                    if u := due(at, s, 2, "scaled"):
                        wait(pool, q_out, u.count(1, 1))
                        wait(pool, k_out, u.count(1, 1))
                        wait(pool, rope_done, u.count(1, 0))
                        nc.gpsimd.tensor_tensor(
                            scaled[:, :, :].rearrange("p n (b t) -> p (n b) t", b=NB),
                            qk[u.par][0:H * ROT, :, :].rearrange("p n (b t) -> p (n b) t", b=NB),
                            cos_sb[:, :].unsqueeze(1).to_broadcast([H * ROT, 2 * NB, T]),
                            ALU.mult).then_inc(scaled_done, 1)
                    if u := due(at, s, 2, "rope"):
                        wait(pool, scaled_done, u.count(1, 1))
                        wait(pool, turned_done, u.count(2, 2))
                        nc.gpsimd.tensor_tensor(qk[u.par][0:H * ROT, :, :], scaled[:, :, :], turned[:, :, :],
                                                ALU.add).then_inc(rope_done, 1)
                    if u := due(at, s, 2, "rest1"):
                        wait(pool, p1_done, u.count(1, 1))
                        nc.gpsimd.tensor_tensor(qk[u.par][:, :, :], qk[u.par][:, :, :], parts[:, 0:6:3, :],
                                                ALU.subtract).then_inc(r1_done, 1)
                    if u := due(at, s, 2, "part3"):
                        wait(pool, p2_done, u.count(1, 1))
                        nc.gpsimd.tensor_tensor(parts[:, 2:6:3, :], qk[u.par][:, :, :], parts[:, 1:6:3, :],
                                                ALU.subtract).then_inc(p3_done, 1)
                    if u := due(at, s, 3, "rs1"):
                        inverse_deviation(u, mv1, ve1, rs1, mv1_done, ve1_done, rs1_done, xn_done)
                    for f in range(FCH):
                        if u := due(at, s, -2, "low", f):
                            low_half(u, f)
                    if u := due(at, s, -1, "gated"):
                        wait(pool, oc_in, u.count(64, 64))
                        wait(pool, rec_in, u.count(64, 64))
                        wait(pool, wo_mm, u.count(1, 0))
                        nc.gpsimd.tensor_tensor(on[:, :], oc[:, :], rec[:, :], ALU.mult
                                                ).then_inc(on_done, 1)
                    if u := due(at, s, -1, "x2"):
                        wait(pool, attn_out, u.count(1, 1))
                        wait(pool, xr_in[u.par], u.pair_count(16, 16))
                        wait(pool, fo_done, u.count(1, -1))
                        nc.gpsimd.tensor_tensor(
                            x2[u.par][:, :, :], xr[u.par][:, :, :],
                            attn[:, :].rearrange("p (b t) -> p b t", b=NB), ALU.add
                        ).then_inc(x2_done, 1)
                    if u := due(at, s, -2, "rs2"):
                        inverse_deviation(u, mv2, ve2, rs2, mv2_done, ve2_done, rs2_done, xn2_done)

            iterations(pool, body, once)

        @block.scalar
        def _(act):
            def once(i):
                if i == -LEAD:
                    act.wait_ge(s_small, 16 * 6)
                    nc.scalar.activation(gate_x[:, :], gates[:, 0:1], ACT.Tanh).then_inc(s_gate, 1)
                    nc.scalar.activation(gate_f[:, :], gates[:, 1:2], ACT.Tanh).then_inc(s_gate, 1)
                if i == -2:
                    act.wait_ge(s_const, 4)
                if i == -1:
                    act.wait_ge(s_split, 2)
                if i == 0:
                    act.wait_ge(s_bias, 1)

            def rectify(u, f):
                wait(act, fc_mm, u.count(FCH, f + 1))
                wait(act, hid_done, u.count(FCH, f - 1))
                nc.scalar.activation(
                    relu[f % 2][:, :, :], (gb, ga, gb, ga)[f][:, :].rearrange("p (n c) -> p n c", n=2),
                    ACT.Relu).then_inc(relu_done, 1)

            def square(u, f):
                wait(act, relu_done, u.count(FCH, f + 1))
                wait(act, lo_done, u.count(FCH, f - 1))
                nc.scalar.activation(hid[f % 2][:, :, :], relu[f % 2][:, :, :], ACT.Square
                                     ).then_inc(hid_done, 1)

            def high_half(u, f):
                wait(act, hid_done, u.count(FCH, f + 1))
                wait(act, proj_mm, u.count(FCH, f + 1 - FCH))
                nc.scalar.activation(hid_hi[:, f, :, :], hid[f % 2][:, :, :], ACT.Copy
                                     ).then_inc(hi_done, 1)

            def body(at):
                for s in range(SLOTS):
                    if u := due(at, s, 2, "q_out"):
                        wait(act, q_mm, u.count(1, 1))
                        wait(act, p3_done, u.count(1, -1))
                        nc.scalar.activation(qk[u.par][:, 0, :], ga[:, :], ACT.Identity,
                                             bias=bq_sb[:, :]).then_inc(q_out, 1)
                    if u := due(at, s, 2, "k_out"):
                        wait(act, k_mm, u.count(1, 1))
                        nc.scalar.activation(qk[u.par][:, 1, :], gb[:, :], ACT.Identity,
                                             bias=bk_sb[:, :]).then_inc(k_out, 1)
                    if u := due(at, s, 2, "part1"):
                        wait(act, rope_done, u.count(1, 1))
                        wait(act, q_out, u.count(1, 1))
                        wait(act, k_out, u.count(1, 1))
                        other = Unit(u.r, u.k - 1)
                        for b in range(NB):
                            wait(act, stacked[other.par][b], other.pair_count(96, 96))
                        nc.scalar.activation(parts[:, 0:6:3, :], qk[u.par][:, :, :], ACT.Copy
                                             ).then_inc(p1_done, 1)
                    if u := due(at, s, 2, "part2"):
                        wait(act, r1_done, u.count(1, 1))
                        nc.scalar.activation(parts[:, 1:6:3, :], qk[u.par][:, :, :], ACT.Copy
                                             ).then_inc(p2_done, 1)
                    if u := due(at, s, 1, "v_out"):
                        wait(act, v_mm, u.count(1, 1))
                        wait(act, pv_mm, u.count(GROUPS, -GROUPS))
                        nc.scalar.activation(
                            vp[u.par][:, :, :, 0:D], ga[:, :].rearrange("p (n h i) -> p n h i", h=H, i=D),
                            ACT.Copy).then_inc(v_out, 1)
                    if u := due(at, s, -3, "y_out"):
                        wait(act, proj_mm, u.count(FCH, FCH))
                        wait(act, count_step, u.count(STEPS, 0))
                        nc.scalar.activation(y_sb[:, :], y_bank[:, :], ACT.Copy).then_inc(y_out, 1)
                    if u := due(at, s, -2, "xh"):
                        wait(act, xt_mm, u.count(1, 1))
                        wait(act, fc_mm, u.count(FCH, -FCH))
                        nc.scalar.activation(
                            xh[u.par][:, :, :], ga[:, :].rearrange("p (n c) -> p n c", n=2), ACT.Copy
                        ).then_inc(xh_done, 1)
                    for f in range(FCH):
                        if u := due(at, s, -2, "relu", f):
                            rectify(u, f)
                        if u := due(at, s, -2, "square", f):
                            square(u, f)
                        if u := due(at, s, -2, "high", f):
                            high_half(u, f)
                    if u := due(at, s, -1, "attn"):
                        wait(act, wo_mm, u.count(1, 1))
                        wait(act, x2_done, u.count(1, 0))
                        nc.scalar.activation(attn[:, :], ga[:, :], ACT.Identity,
                                             scale=gate_x[:, :], bias=bias_o[:, :]).then_inc(attn_out, 1)
                    for n in range(ITEMS):
                        if u := due(at, s, 0, "exp", n):
                            wait(act, score_mm, u.count(ITEMS, n + 1))
                            if n % 4 == 0:
                                wait(act, pv_mm, u.count(GROUPS, n // 4 - 1))
                            nc.scalar.activation(
                                probs[:, n % 8, :, :],
                                score_bank[n % 2][:, :].rearrange("p (n t) -> p n t", n=2),
                                ACT.Exp, scale=1.0 / D ** 0.5).then_inc(exp_done, 1)
                    for b in range(NB):
                        if u := due(at, s, 0, "u_out", b):
                            copy_u(u, b)

            def copy_u(u, b):
                wait(act, pv_mm, u.count(GROUPS, 2 * b + 2))
                if b == 0:
                    wait(act, sums_in, u.count(64, 0))
                    wait(act, oc_in, u.count(64, 0))
                nc.scalar.activation(usb[:, :, b, :], u_bank[:, :].rearrange("p (g t) -> p g t", g=2),
                                     ACT.Copy).then_inc(u_out, 1)

            iterations(act, body, once)

        @block.vector
        def _(dve):
            def once(i):
                if i == -LEAD:
                    nc.vector.memset(ones(0), 1.0).then_inc(s_const, 1)
                    dve.wait_ge(s_w, 16 * 5)
                if i == -2:
                    nc.vector.memset(ones(1), 1.0).then_inc(s_const, 1)
                    dve.wait_ge(s_bvo, 1)
                    dve.wait_ge(s_small, 16 * 6)
                    nc.vector.tensor_tensor(bias_t[:, :], y_bank[:, 0:1], bo_sb[:, :], ALU.add
                                            ).then_inc(s_gscaled, 1)
                    dve.wait_ge(s_gate, 2)
                    dve.wait_ge(s_gscaled, 1)
                    nc.vector.tensor_tensor(bias_o[:, :], bias_t[:, :], gate_x[:, :], ALU.mult
                                            ).then_inc(s_bias, 1)
                    nc.vector.tensor_scalar(gates[:, 1:2], gate_f[:, :], 1.0 / STEPS, None, ALU.mult
                                            ).then_inc(s_gscaled, 1)
                if i == -1:
                    split(wfc_sb, wfc_hi, wfc_lo, 0)
                if i == 0:
                    split(wproj_sb, wproj_hi, wproj_lo, 1)
                    dve.wait_ge(s_gscaled, 2)

            def ones(p):
                return stack[p][KROWS:KROWS + 3, :, :, 1, :]

            def split(raw, hi, lo, n):
                dve.wait_ge(s_ffn, 32)
                nc.vector.tensor_copy(hi[:, :, :], raw[:, :, :]).then_inc(s_split, 1)
                dve.wait_ge(s_split, 2 * n + 1)
                nc.vector.tensor_tensor(lo[:, :, :], raw[:, :, :], hi[:, :, :].bitcast(F32),
                                        ALU.subtract).then_inc(s_split, 1)

            def statistics(u, src, st, mv, st_done, mv_done, norm_done):
                for b in range(NB):
                    last = nc.vector.bn_stats(st[:, b, :], src[:, b, :])
                last.then_inc(st_done, 1)
                wait(dve, st_done, u.count(1, 1))
                nc.vector.memset(fence[:, :], 0.0)
                for b in range(NB):
                    last = nc.vector.bn_aggr(mv[:, b, :], st[:, b, :])
                last.then_inc(mv_done, 1)

            def normalize(u, dst, src, mv, rs, rs_done, done):
                wait(dve, rs_done, u.count(1, 1))
                for b in range(NB):
                    last = nc.vector.tensor_scalar(dst[:, b, :], src[:, b, :], mv[:, b, 0:1],
                                                   rs[:, b:b + 1], ALU.subtract, ALU.mult)
                last.then_inc(done, 1)

            def count_spikes(u, n):
                y = y_sb[:, :]
                if n == 0:
                    wait(dve, y_out, u.count(1, 1))
                    wait(dve, fo_done, u.count(1, 0))
                    nc.vector.tensor_scalar(cnt[0][:, :], y, thresholds[0], None, ALU.is_gt
                                            ).then_inc(count_step, 1)
                    return
                wait(dve, count_step, u.count(STEPS, n))
                if n < STEPS:
                    nc.vector.scalar_tensor_tensor(
                        out=cnt[n % 2][:, :], in0=y, scalar=thresholds[n],
                        in1=cnt[(n - 1) % 2][:, :], op0=ALU.is_gt, op1=ALU.add).then_inc(count_step, 1)
                    return
                wait(dve, stored[u.par], u.pair_count(16, 0))
                nc.vector.scalar_tensor_tensor(
                    out=fo[u.par][:, :, :],
                    in0=cnt[(STEPS - 1) % 2][:, :].rearrange("p (b t) -> p b t", b=NB),
                    scalar=gates[:, 1:2], in1=x2[u.par][:, :, :], op0=ALU.mult, op1=ALU.add
                ).then_inc(fo_done, 1)

            def max_parts(u):
                wait(dve, mt_mm, u.count(1, 1))
                other = Unit(u.r, u.k - 1)
                wait(dve, m_stacked[other.par], other.pair_count(48, 48))
                m = gb[0:ITEMS, 0:T]
                nc.vector.tensor_copy(mparts[:, 0, :], m).then_inc(m1_done, 1)
                wait(dve, m1_done, u.count(1, 1))
                nc.vector.tensor_tensor(mrest[:, :], m, mparts[:, 0, :], ALU.subtract
                                        ).then_inc(mr_done, 1)
                wait(dve, mr_done, u.count(1, 1))
                nc.vector.tensor_copy(mparts[:, 1, :], mrest[:, :]).then_inc(m2_done, 1)
                wait(dve, m2_done, u.count(1, 1))
                nc.vector.tensor_tensor(mparts[:, 2, :], mrest[:, :], mparts[:, 1, :],
                                        ALU.subtract).then_inc(m3_done, 1)

            def body(at):
                for s in range(SLOTS):
                    if u := due(at, s, -1, "recip"):
                        wait(dve, sums_in, u.count(64, 64))
                        wait(dve, rsums_out, u.count(16, 0))
                        nc.vector.reciprocal(rsums[:, :], sums[:, :]).then_inc(rsums_done, 1)
                    for n in range(ITEMS):
                        if u := due(at, s, 1, "take_max", n):
                            if n == 0:
                                wait(dve, mt_mm, u.count(1, -1))
                            wait(dve, max_mm, u.count(ITEMS, n + 1))
                            nc.vector.tensor_reduce(
                                mx[u.par][:, :, n // H, n % H],
                                max_bank[n % 2][:, :].rearrange("p (n t) -> p n t", n=2),
                                AX.X, ALU.max, negate=True).then_inc(max_done, 1)
                    if u := due(at, s, 1, "max_parts"):
                        max_parts(u)
                    for n, (src, dst) in enumerate(((H * ROT // 2, 0), (0, H * ROT // 2))):
                        if u := due(at, s, 2, "turned", n):
                            half = H * ROT // 2
                            if n == 0:
                                wait(dve, q_out, u.count(1, 1))
                                wait(dve, k_out, u.count(1, 1))
                                wait(dve, rope_done, u.count(1, 0))
                            nc.vector.tensor_tensor(
                                turned[dst:dst + half, :, :].rearrange("p n (b t) -> p (n b) t", b=NB),
                                qk[u.par][src:src + half, :, :].rearrange("p n (b t) -> p (n b) t", b=NB),
                                sin_sb[src:src + half, :].unsqueeze(1).to_broadcast([half, 2 * NB, T]),
                                ALU.mult).then_inc(turned_done, 1)
                    if u := due(at, s, -2, "stats2"):
                        wait(dve, x2_done, u.count(1, 1))
                        wait(dve, xn2_done, u.count(1, 0))
                        statistics(u, x2[u.par], st2, mv2, st2_done, mv2_done, xn2_done)
                    if u := due(at, s, -2, "norm2"):
                        wait(dve, xt_mm, u.count(1, 0))
                        normalize(u, xn2, x2[u.par], mv2, rs2, rs2_done, xn2_done)
                    if u := due(at, s, -2, "xl"):
                        wait(dve, xh_done, u.count(1, 1))
                        nc.vector.tensor_tensor(
                            xl[u.par][:, :, :], ga[:, :].rearrange("p (n c) -> p n c", n=2),
                            xh[u.par][:, :, :].bitcast(F32), ALU.subtract).then_inc(xl_done, 1)
                    for n in range(STEPS + 1):
                        if u := due(at, s, -3, "count", n):
                            count_spikes(u, n)
                    if u := due(at, s, 3, "stats1"):
                        wait(dve, x_in[u.par], u.pair_count(16, 16))
                        wait(dve, xn_done, u.count(1, 0))
                        statistics(u, xa[u.par], st1, mv1, st1_done, mv1_done, xn_done)
                    if u := due(at, s, 3, "norm1"):
                        wait(dve, q_mm, u.count(1, -1))
                        normalize(u, xn[u.par], xa[u.par], mv1, rs1, rs1_done, xn_done)

            iterations(dve, body, once)

        @block.tensor
        def _(pe):
            def once(i):
                if i == -LEAD:
                    pe.wait_ge(s_wqk, 32)
                if i == -2:
                    pe.wait_ge(s_w, 16 * 5)
                    pe.wait_ge(s_small, 16 * 6)
                    nc.tensor.matmul(y_bank[:, 0:1], wo_sb[:, :], bv_sb[:, :], start=True, stop=True
                                     ).then_inc(s_bvo, 1)
                    pe.wait_ge(s_const, 4)
                if i == 1:
                    pe.wait_ge(s_split, 4)
                    pe.wait_ge(s_gscaled, 2)

            def wait_peeled(u, sem, value):
                if u.fixed:
                    wait(pe, sem, value)

            def other(u, ahead):
                return Unit(u.r, u.k + ahead)

            def project_q(u):
                p = u.par
                wait(pe, xn_done, u.count(1, 1))
                wait(pe, attn_out, other(u, -4).count(1, 1))
                wait_peeled(u, relu_done, other(u, -5).count(FCH, FCH))
                wait_peeled(u, v_out, other(u, -2).count(1, 1))
                nc.tensor.matmul(ga[:, :], wq_sb[:, :], xn[p][:, :, :].rearrange("c b t -> c (b t)"),
                                 start=True, stop=True).then_inc(q_mm, 1)

            def project_k(u):
                p = u.par
                wait(pe, c_in[p], u.pair_count(16, 16))
                wait(pe, mr_done, other(u, -2).count(1, 1))
                wait_peeled(u, k_out, other(u, -1).count(1, 1))
                nc.tensor.matmul(gb[:, :], wk_sb[:, :], ca[p][:, :, :].rearrange("c b t -> c (b t)"),
                                 start=True, stop=True).then_inc(k_mm, 1)

            def project_v(u):
                p = u.par
                wait(pe, q_out, other(u, 1).count(1, 1))
                wait_peeled(u, attn_out, other(u, -3).count(1, 1))
                wait_peeled(u, relu_done, other(u, -4).count(FCH, FCH))
                wait(pe, c_in[p], u.pair_count(16, 16))
                for n in range(2 * NB):
                    last = nc.tensor.matmul(ga[:, n * C:(n + 1) * C],
                                            ca[p][:, n // 2, (n % 2) * 128:(n % 2) * 128 + 128],
                                            wv_sb[:, :], start=True, stop=True)
                last.then_inc(v_mm, 1)

            def project_out(u):
                wait(pe, on_done, u.count(1, 1))
                wait(pe, relu_done, other(u, -1).count(FCH, FCH))
                wait_peeled(u, v_out, other(u, 2).count(1, 1))
                nc.tensor.matmul(ga[:, :], wo_sb[:, :], on[:, :], start=True, stop=True).then_inc(wo_mm, 1)

            def turn(u):
                wait(pe, xn2_done, u.count(1, 1))
                wait(pe, v_out, other(u, 3).count(1, 1))
                wait_peeled(u, attn_out, u.count(1, 1))
                wait_peeled(u, relu_done, other(u, -1).count(FCH, FCH))
                for dc in range(2):
                    for b in range(NB):
                        o = (dc * NB + b) * 128
                        last = nc.tensor.transpose(ga[:, o:o + 128], xn2[:, b, dc * 128:(dc + 1) * 128],
                                                   eye_sb[:, :])
                last.then_inc(xt_mm, 1)

            def turn_max(u):
                wait(pe, max_done, u.count(ITEMS, ITEMS))
                wait(pe, relu_done, other(u, -3).count(FCH, 3))
                wait_peeled(u, k_out, other(u, 1).count(1, 1))
                for half in range(2):
                    last = nc.tensor.transpose(gb[0:ITEMS, half * 128:half * 128 + 128],
                                               mx[u.par][:, half, :, :].rearrange("p b h -> p (b h)"),
                                               eye_sb[:, :])
                last.then_inc(mt_mm, 1)

            def max_item(u, n):
                b, h = n // H, n % H
                q, k = stack[u.par][:, b, h, 0, :], stack[u.par][:, b, h, 1, :]
                if h == 0:
                    wait(pe, stacked[u.par][b], u.pair_count(96, 96))
                wait(pe, max_done, u.count(ITEMS, n - 1))
                for half in range(2):
                    last = nc.tensor.matmul(max_bank[n % 2][:, half * T:(half + 1) * T],
                                            q[0:KROWS, half * 128:half * 128 + 128], k[0:KROWS, :],
                                            start=True, stop=True)
                last.then_inc(max_mm, 1)

            def score_item(u, n):
                b, h = n // H, n % H
                q, k = stack[u.par][:, b, h, 0, :], stack[u.par][:, b, h, 1, :]
                if n == 0:
                    wait(pe, m_stacked[u.par], u.pair_count(48, 48))
                wait(pe, exp_done, u.count(ITEMS, n - 1))
                for half in range(2):
                    last = nc.tensor.matmul(score_bank[n % 2][:, half * T:(half + 1) * T],
                                            k[0:KROWS + 3, half * 128:half * 128 + 128],
                                            q[0:KROWS + 3, :], start=True, stop=True)
                last.then_inc(score_mm, 1)

            def v_products(u, g):
                b, top = g // 2, g % 2
                wait(pe, exp_done, u.count(ITEMS, 4 * g + 4))
                if g == 0:
                    wait(pe, v_out, u.count(1, 1))
                if top == 0:
                    wait(pe, u_out, u.count(2, b))
                for half in range(2):
                    for j in range(4):
                        last = nc.tensor.matmul(
                            u_bank[32 * j:32 * j + 32, top * T:(top + 1) * T],
                            vp[u.par][:, 2 * b + half, 4 * top + j, :],
                            probs[:, (4 * g + j) % 8, half, :], start=(half == 0), stop=(half == 1))
                last.then_inc(pv_mm, 1)

            def first_product(u, f):
                p = u.par
                if f == 0:
                    wait(pe, xl_done, u.count(1, 1))
                    wait(pe, k_out, other(u, 4).count(1, 1))
                    wait_peeled(u, mr_done, other(u, 2).count(1, 1))
                    wait_peeled(u, relu_done, u.count(FCH, 0))
                if f == 2:
                    wait(pe, relu_done, u.count(FCH, 1))
                if f == 3:
                    wait(pe, relu_done, u.count(FCH, 2))
                dst = (gb, ga, gb, ga)[f]
                for half in range(2):
                    f0 = (2 * f + half) * 128
                    n = 0
                    for dc in range(2):
                        for w, xx in ((wfc_hi, xh), (wfc_hi, xl), (wfc_lo, xh)):
                            last = nc.tensor.matmul(dst[:, half * 256:half * 256 + 256],
                                                    w[:, dc, f0:f0 + 128], xx[p][:, dc, :],
                                                    start=(n == 0), stop=(n == 5))
                            n += 1
                last.then_inc(fc_mm, 1)

            def second_product(u, f, half):
                if half == 0:
                    wait(pe, lo_done, u.count(FCH, f + 1))
                    if f == 0:
                        wait(pe, y_out, u.count(1, 0))
                for b in range(NB):
                    for n, (hh, w) in enumerate(((hid_hi, wproj_hi), (hid_lo, wproj_hi), (hid_hi, wproj_lo))):
                        last = nc.tensor.matmul(
                            y_bank[:, b * T:(b + 1) * T], hh[:, f, half, b * C:(b + 1) * C],
                            w[:, 2 * f + half, :], start=(f == 0 and half == 0 and b == 0 and n == 0),
                            stop=(f == FCH - 1 and half == 1 and n == 2), skip_group_check=True)
                if half == 1:
                    last.then_inc(proj_mm, 1)

            def body(at):
                for s in range(SLOTS):
                    for n in range(ITEMS):
                        if u := due(at, s, 1, "max", n):
                            max_item(u, n)
                    for n in range(ITEMS):
                        if u := due(at, s, 0, "score", n):
                            score_item(u, n)
                    for g in range(GROUPS):
                        if u := due(at, s, 0, "v_product", g):
                            v_products(u, g)
                    for ahead, step, product in ((2, "q", project_q), (2, "k", project_k),
                                                 (1, "v", project_v), (-2, "turn", turn)):
                        if u := due(at, s, ahead, step):
                            product(u)
                    for f in range(FCH):
                        if u := due(at, s, -2, "fc", f):
                            first_product(u, f)
                    for n in range(2 * FCH):
                        if u := due(at, s, -2, "proj", n):
                            second_product(u, n // 2, n % 2)
                    for ahead, step, product in ((-1, "wo", project_out), (1, "turn_max", turn_max)):
                        if u := due(at, s, ahead, step):
                            product(u)

            iterations(pe, body, once)


_NAMES = ("x", "ctx", "gx", "gf", "wq", "wk", "wv", "wo", "bq", "bk", "bv", "bo", "wfc", "wproj",
          "cos", "sin", "eye")


def kernel(x, ctx_1024, g_xattn, g_ffn, L0_xattn_Wq, L0_xattn_bq, L0_xattn_Wk, L0_xattn_bk,
           L0_xattn_Wv, L0_xattn_bv, L0_xattn_Wo, L0_xattn_bo, L0_ffn_W_fc, L0_ffn_W_proj):
    import concourse.bacc as bacc
    from concourse.bass_utils import run_bass_kernel_spmd as run

    order = np.arange(C).reshape(H, D).T.reshape(-1)
    out_order = np.arange(C).reshape(2, 4, D).transpose(1, 2, 0).reshape(-1)
    wq, wk, wv, wo = (np.asarray(w) for w in (L0_xattn_Wq, L0_xattn_Wk, L0_xattn_Wv, L0_xattn_Wo))

    theta = (1.0 / np.float32(2500) ** (np.arange(0, ROT, 2, dtype=np.float32) / np.float32(ROT))
             ).astype(np.float32)
    angle = np.arange(T, dtype=np.float32)[None, :] * theta[:, None]
    cos = np.repeat(np.cos(angle), H, axis=0)
    sin = np.repeat(np.sin(angle), H, axis=0)
    arrays = {
        "x": np.asarray(x), "ctx": np.asarray(ctx_1024), "gx": np.asarray(g_xattn), "gf": np.asarray(g_ffn),
        "wq": wq[order].T, "wk": wk[order].T, "wv": wv.T, "wo": wo.T[out_order],
        "bq": np.asarray(L0_xattn_bq)[order], "bk": np.asarray(L0_xattn_bk)[order],
        "bv": np.asarray(L0_xattn_bv)[out_order], "bo": np.asarray(L0_xattn_bo),
        "wfc": np.asarray(L0_ffn_W_fc).T, "wproj": np.asarray(L0_ffn_W_proj).T,
        "cos": np.concatenate([cos, cos]), "sin": np.concatenate([sin, -sin]),
        "eye": np.eye(128, dtype=np.float32),
    }
    arrays = {f"in_{n}": np.ascontiguousarray(arrays[n], dtype=np.float32) for n in _NAMES}
    nc = bacc.Bacc("TRN2", target_bir_lowering=False, num_devices=1)
    args = [nc.dram_tensor(n, a.shape, F32, kind="ExternalInput").ap() for n, a in arrays.items()]
    out = nc.dram_tensor("out_0", (B, C, T), F32, kind="ExternalOutput").ap()
    scratch = nc.dram_tensor("scratch", (4, 2, W), F32, kind="Internal").ap()
    build(nc, *args, out, scratch)
    r = run(nc, [arrays], core_ids=[0])
    return r.results[0]["out_0"]
```

```python
import numpy as np
import concourse.bass as bass
from concourse import mybir
from contextlib import ExitStack

F32 = mybir.dt.float32
F32R = mybir.dt.float32r
BF16 = mybir.dt.bfloat16
ALU = mybir.AluOpType
ACT = mybir.ActivationFunctionType
AX = mybir.AxisListType

B, C, T = 64, 128, 256
H, D = 8, 16
ROT = D // 2
FF = 4 * T
NB = 2
UNITS = B // NB
W = NB * T
ITEMS = NB * H
GROUPS = ITEMS // 4
FCH = FF // 128 // 2
BETA, THRESHOLD, STEPS = 0.9, 1.0, 5
EPS = 1e-5
Q_PARTS = (0, 0, 0, 1, 1, 2)
K_PARTS = (0, 1, 2, 0, 1, 0)
KROWS = 6 * D

LEAD, LAG = 3, 3


def spike_thresholds():
    f = np.float32

    def spikes(y):
        mem, count = f(0), 0
        for _ in range(STEPS):
            reset = f(mem - f(THRESHOLD) > 0)
            mem = f(f(f(f(BETA) * mem) + y) - f(reset * f(THRESHOLD)))
            count += int(mem - f(THRESHOLD) > 0)
        return count

    found = []
    for n in range(1, STEPS + 1):
        low, high = int(f(0).view(np.uint32)), int(f(4).view(np.uint32))
        while high - low > 1:
            mid = (low + high) // 2
            if spikes(np.uint32(mid).view(f)) >= n:
                high = mid
            else:
                low = mid
        found.append(float(np.uint32(low).view(f)))
    return found


class Unit:

    def __init__(self, r, k):
        self.r, self.k = r, k
        self.par = k % 2
        self.fixed = isinstance(r, int)

    def exists(self):
        return not self.fixed or 0 <= 2 * self.r + self.k < UNITS

    def number(self):
        return 2 * self.r + self.k

    def count(self, per, plus):
        n = 2 * per * self.r + (per * self.k + plus)
        return min(n, per * UNITS) if self.fixed else n

    def pair_count(self, per, plus):
        n = per * self.r + (per * (self.k // 2) + plus)
        return n


def wait(eng, sem, value):
    if isinstance(value, int) and value <= 0:
        return
    eng.wait_ge(sem, value)


def wait_apart(eng, sem, value, met):
    if isinstance(value, int):
        wait(eng, sem, value)
        return
    value = eng.snap(value)
    eng.wait_ge(met, 16)
    eng.wait_ge(sem, value)


SLOTS = 64
SCHEDULE = {
    "q": [0], "k": [2], "v": [7], "max": [2, 2, 6, 8, 12, 16, 18, 22, 26, 28, 32, 34, 39, 42, 46, 48],
    "turn_max": [51], "score": [9, 14, 18, 22, 26, 28, 30, 34, 38, 40, 44, 46, 50, 54, 56, 61],
    "v_product": [30, 44, 56, 67], "wo": [55], "turn": [16], "fc": [28, 34, 41, 46],
    "proj": [46, 49, 66, 66, 70, 71, 76, 79],
    "q_out": [3], "k_out": [4], "part1": [20], "part2": [28], "v_out": [4], "ctx_high": [26],
    "xn_high": [42], "exp": [17, 19, 23, 25, 27, 27, 31, 34, 39, 40, 44, 46, 52, 54, 56, 58],
    "u_out": [44, 71], "attn": [56], "xh": [24], "relu": [33, 36, 42, 46], "square": [36, 40, 46, 54],
    "high": [39, 44, 52, 58], "y_out": [21],
    "ctx_low": [40], "rs1": [25], "scaled": [13], "rope": [16], "rest1": [20], "part3": [31],
    "gated": [47], "x2": [55], "rs2": [14], "low": [38, 47, 52, 56],
    "stats1": [26], "norm1": [38], "xn_low": [49], "turned": [2, 2],
    "take_max": [0, 2, 6, 8, 12, 16, 18, 22, 26, 28, 32, 38, 38, 46, 46, 48], "max_parts": [60],
    "recip": [26], "stats2": [0], "norm2": [10], "xl": [22], "count": [24, 30, 30, 36, 42, 46],
    "load_x": [0], "load_ctx": [2], "load_residual": [4], "stack": [47, 56], "stack_max": [52],
    "move_sums": [2], "move_v": [11], "put_sums": [12], "spread_sums": [22], "store": [49],
}


def due(at, s, ahead, step, n=0):
    slot = SCHEDULE[step][n]
    u = at(ahead - slot // SLOTS)
    return u if slot % SLOTS == s and u.exists() else None


def build(nc, x, ctx_in, gx, gf, wq, wk, wv, wo, bq, bk, bv, bo, wfc, wproj, cos, sin, eye, out,
          scratch):
    thresholds = spike_thresholds()
    x_u = x.rearrange("(u b) c t -> u c b t", b=NB)
    c_u = ctx_in.rearrange("(u b) c t -> u c b t", b=NB)
    out_u = out.rearrange("(u b) c t -> u c b t", b=NB)

    ctx = ExitStack()
    with ctx:
        def sb(name, shape, dt=F32):
            return ctx.enter_context(nc.sbuf_tensor(name, shape, dt))

        def two(name, shape, dt=F32):
            return [sb(f"{name}{i}", shape, dt) for i in range(2)]

        def bank(name):
            return ctx.enter_context(nc.psum_tensor(name, [128, 512], F32))

        def sem(name):
            return ctx.enter_context(nc.semaphore(name))

        wqk_sb = sb("wqk_sb", [C, 2, C])
        wqk_hi, wqk_lo = sb("wqk_hi", [C, 2, C], F32R), sb("wqk_lo", [C, 2, C], F32R)
        wv_sb, wo_sb = sb("wv_sb", [C, C]), sb("wo_sb", [C, C])
        eye_sb = sb("eye_sb", [128, 128])
        wfc_hi, wfc_lo = sb("wfc_hi", [128, 2, FF], F32R), sb("wfc_lo", [128, 2, FF], F32R)
        wproj_hi, wproj_lo = (sb(n, [128, FF // 128, T], F32R) for n in ("wproj_hi", "wproj_lo"))
        cos_sb, sin_sb = sb("cos_sb", [H * ROT, T]), sb("sin_sb", [H * ROT, T])
        bq_sb, bk_sb, bv_sb, bo_sb = (sb(n, [C, 1]) for n in ("bq_sb", "bk_sb", "bv_sb", "bo_sb"))
        gates = sb("gates", [128, 2])
        gate_x, gate_f = sb("gate_x", [128, 1]), sb("gate_f", [128, 1])
        bias_o = sb("bias_o", [128, 1])
        bias_t = sb("bias_t", [128, 1])
        minus_half, eps_sb = sb("minus_half", [128, NB]), sb("eps_sb", [128, NB])
        fence = sb("fence", [1, 1])

        xa, xr = two("xa", [128, NB, T]), two("xr", [128, NB, T])
        x2, fo = two("x2", [128, NB, T]), two("fo", [128, NB, T])
        xn, ca = sb("xn", [128, NB, T]), two("ca", [128, NB, T])
        xn_hi, xn_lo = sb("xn_hi", [128, NB, T], F32R), sb("xn_lo", [128, NB, T], F32R)
        ca_hi, ca_lo = sb("ca_hi", [128, NB, T], F32R), sb("ca_lo", [128, NB, T], F32R)
        st1, mv1, ve1, rs1 = (sb("st1", [128, NB, 6]), sb("mv1", [128, NB, 2]),
                              sb("ve1", [128, NB]), sb("rs1", [128, NB]))
        st2, mv2, ve2, rs2 = (sb("st2", [128, NB, 6]), sb("mv2", [128, NB, 2]),
                              sb("ve2", [128, NB]), sb("rs2", [128, NB]))
        qk = two("qk", [128, 2, W])
        turned = sb("turned", [H * ROT, 2, W])
        scaled = sb("scaled", [H * ROT, 2, W])
        parts = sb("parts", [128, 6, W], BF16)
        stack = two("stack", [128, NB, H, 2, T], BF16)
        vp = two("vp", [128, 2 * NB, H, 2 * D])
        mx = two("mx", [128, 2, NB, H])
        mparts = sb("mparts", [ITEMS, 3, T], BF16)
        mrest = sb("mrest", [ITEMS, T])
        probs = sb("probs", [128, 8, 2, T])
        wfc_sb = probs[:, 0:4, :, :].rearrange("p a n t -> p (a n t)").rearrange("p (n f) -> p n f", n=2)
        usb = sb("usb", [128, 2, NB, T])
        oc, rec = sb("oc", [128, W]), sb("rec", [128, W])
        sums, rsums = sb("sums", [128, 8 * W // 128]), sb("rsums", [128, 8 * W // 128])
        on = sb("on", [128, W])
        attn = sb("attn", [128, W])
        xn2 = sb("xn2", [128, NB, T])
        xh, xl = two("xh", [128, 2, NB * C], F32R), two("xl", [128, 2, NB * C], F32R)
        hidden = sb("hidden", [128, 8, NB * C])
        relu, hid = [hidden[:, 0:2, :], hidden[:, 2:4, :]], [hidden[:, 4:6, :], hidden[:, 6:8, :]]
        wproj_sb = hidden[:, :, 0:T]
        hid_hi, hid_lo = (sb(n, [128, FCH, 2, NB * C], F32R) for n in ("hid_hi", "hid_lo"))
        y_sb = sb("y_sb", [128, W])
        cnt = two("cnt", [128, W])

        score_bank = [bank("score0"), bank("score1")]
        max_bank = [bank("max0"), bank("max1")]
        u_bank, y_bank = bank("u_bank"), bank("y_bank")
        ga, gb = bank("ga"), bank("gb")

        s_wqk, s_w, s_small, s_ffn = sem("s_wqk"), sem("s_w"), sem("s_small"), sem("s_ffn")
        s_const, s_split, s_gate, s_bvo, s_bias = (sem("s_const"), sem("s_split"), sem("s_gate"),
                                                   sem("s_bvo"), sem("s_bias"))
        s_gscaled, s_half = sem("s_gscaled"), sem("s_half")
        x_in, c_in, xr_in = ([sem(f"{n}{i}") for i in range(2)] for n in ("x_in", "c_in", "xr_in"))
        xn_hi_done, xn_lo_done, ca_hi_done, ca_lo_done, s_qk = (
            sem(n) for n in ("xn_hi_done", "xn_lo_done", "ca_hi_done", "ca_lo_done", "s_qk"))
        st1_done, mv1_done, ve1_done, rs1_done, xn_done = (
            sem(n) for n in ("st1_done", "mv1_done", "ve1_done", "rs1_done", "xn_done"))
        st2_done, mv2_done, ve2_done, rs2_done, xn2_done = (
            sem(n) for n in ("st2_done", "mv2_done", "ve2_done", "rs2_done", "xn2_done"))
        q_mm, k_mm, v_mm = sem("q_mm"), sem("k_mm"), sem("v_mm")
        q_out, k_out, v_out = sem("q_out"), sem("k_out"), sem("v_out")
        turned_done, scaled_done, rope_done = sem("turned_done"), sem("scaled_done"), sem("rope_done")
        p1_done, r1_done, p2_done, p3_done = (sem(n) for n in ("p1_done", "r1_done", "p2_done", "p3_done"))
        stacked = [[sem(f"stacked{p}{b}") for b in range(NB)] for p in range(2)]
        max_mm, max_done, mt_mm = sem("max_mm"), sem("max_done"), sem("mt_mm")
        m1_done, mr_done, m2_done, m3_done = (sem(n) for n in ("m1_done", "mr_done", "m2_done", "m3_done"))
        m_stacked = [sem("m_stacked0"), sem("m_stacked1")]
        score_mm, exp_done, pv_mm, u_out = sem("score_mm"), sem("exp_done"), sem("pv_mm"), sem("u_out")
        oc_in = sem("oc_in")
        sums_in, rsums_done, rsums_out, rec_in = (
            sem(n) for n in ("sums_in", "rsums_done", "rsums_out", "rec_in"))
        on_done, wo_mm, attn_out, x2_done = (
            sem(n) for n in ("on_done", "wo_mm", "attn_out", "x2_done"))
        xt_mm, xh_done, xl_done = sem("xt_mm"), sem("xh_done"), sem("xl_done")
        fc_mm, relu_done, hid_done, hi_done, lo_done, proj_mm, y_out = (
            sem(n) for n in ("fc_mm", "relu_done", "hid_done", "hi_done", "lo_done", "proj_mm", "y_out"))
        count_step, fo_done = sem("count_step"), sem("fo_done")
        stored = [sem("stored0"), sem("stored1")]

        def iterations(eng, body, once=lambda i: None):
            def at(r, k):
                return lambda ahead: Unit(r, k + ahead)
            first, last = LAG // 2 + 2, (UNITS - LEAD) // 2 - 1
            for i in range(-LEAD, 2 * first):
                body(at(0, i))
                once(i)
            with eng.Fori(first, last + 1) as r:
                for k in range(2):
                    body(at(r, k))
            for i in range(2 * (last + 1), UNITS + LAG):
                body(at(0, i))

        def vector_splits(u):
            return u.fixed and u.number() == 0

        def scale_qk(eng, arith, u):
            wait(eng, q_out, u.count(1, 1))
            wait(eng, k_out, u.count(1, 1))
            wait(eng, rope_done, u.count(1, 0))
            arith.tensor_tensor(
                scaled[:, :, :].rearrange("p n (b t) -> p (n b) t", b=NB),
                qk[u.par][0:H * ROT, :, :].rearrange("p n (b t) -> p (n b) t", b=NB),
                cos_sb[:, :].unsqueeze(1).to_broadcast([H * ROT, 2 * NB, T]),
                ALU.mult).then_inc(scaled_done, 1)

        def rotate_qk(eng, arith, u):
            wait(eng, scaled_done, u.count(1, 1))
            wait(eng, turned_done, u.count(2, 2))
            arith.tensor_tensor(qk[u.par][0:H * ROT, :, :], scaled[:, :, :], turned[:, :, :],
                                ALU.add).then_inc(rope_done, 1)

        def first_rest(eng, arith, u):
            wait(eng, p1_done, u.count(1, 1))
            arith.tensor_tensor(qk[u.par][:, :, :], qk[u.par][:, :, :], parts[:, 0:6:3, :],
                                ALU.subtract).then_inc(r1_done, 1)

        def last_part(eng, arith, u):
            wait(eng, p2_done, u.count(1, 1))
            arith.tensor_tensor(parts[:, 2:6:3, :], qk[u.par][:, :, :], parts[:, 1:6:3, :],
                                ALU.subtract).then_inc(p3_done, 1)

        block = ctx.enter_context(nc.Block())

        @block.sync
        def _(sp):
            def once(i):
                if i == -LEAD:
                    for n, src in enumerate((wq, wk)):
                        sp.dma_start(wqk_sb[:, n, :], src).then_inc(s_wqk, 16)
                    for dst, src in ((bq_sb, bq), (bk_sb, bk), (bv_sb, bv), (bo_sb, bo)):
                        sp.dma_start(dst[:, :], src.rearrange("(c a) -> c a", a=1)).then_inc(s_small, 16)
                    for n, g in enumerate((gx, gf)):
                        sp.dma_start(gates[:, n:n + 1],
                                     g.rearrange("(a n) -> a n", a=1).to_broadcast([128, 1])
                                     ).then_inc(s_small, 16)
                    for dst, src in ((cos_sb, cos), (sin_sb, sin), (wv_sb, wv), (wo_sb, wo), (eye_sb, eye)):
                        sp.dma_start(dst[:, :], src).then_inc(s_w, 16)
                    sp.dma_start(wfc_sb, wfc.rearrange("(n p) f -> p n f", p=128)).then_inc(s_ffn, 16)
                    sp.dma_start(wproj_sb, wproj.rearrange("(n p) f -> p n f", p=128)).then_inc(s_ffn, 16)

            def stack_parts(u, b):
                wait_apart(sp, p3_done, u.count(1, 1), s_w)
                wait_apart(sp, score_mm, u.count(ITEMS, (b + 1) * H - 2 * ITEMS), s_w)
                cols = slice(b * T, (b + 1) * T)
                for n, (qp, kp) in enumerate(zip(Q_PARTS, K_PARTS)):
                    sp.dma_start(stack[u.par][D * n:D * n + D, b, :, :, :],
                                 parts[:, qp:kp + 4:3 + kp - qp, cols]).then_inc(stacked[u.par][b], 16)

            def body(at):
                for s in range(SLOTS):
                    if u := due(at, s, 3, "load_x"):
                        wait_apart(sp, xn_done, u.count(1, -1), s_w)
                        sp.dma_start(xa[u.par][:, :, :], x_u[u.number()]).then_inc(x_in[u.par], 16)
                    if u := due(at, s, 3, "load_ctx"):
                        wait_apart(sp, v_mm, u.count(1, -1), s_w)
                        sp.dma_start(ca[u.par][:, :, :], c_u[u.number()]).then_inc(c_in[u.par], 16)
                    if u := due(at, s, 0, "load_residual"):
                        wait_apart(sp, x2_done, u.count(1, -1), s_w)
                        sp.dma_start(xr[u.par][:, :, :], x_u[u.number()]).then_inc(xr_in[u.par], 16)
                    if u := due(at, s, -1, "move_sums"):
                        wait_apart(sp, u_out, u.count(2, 2), s_w)
                        for j in range(4):
                            sp.dma_start(sums[32 * j:32 * j + 32, :],
                                         usb[32 * j + D:32 * j + D + 1, :, :, :].rearrange("p g b t -> p (g b t)")
                                         ).then_inc(sums_in, 16)
                    if u := due(at, s, -1, "move_v"):
                        wait_apart(sp, u_out, u.count(2, 2), s_w)
                        wait_apart(sp, on_done, u.count(1, 0), s_w)
                        for j in range(4):
                            sp.dma_start(oc[32 * j:32 * j + 32, :],
                                         usb[32 * j:32 * j + D, :, :, :].rearrange("p g b t -> p (g b t)")
                                         ).then_inc(oc_in, 16)
                    if u := due(at, s, -1, "put_sums"):
                        wait_apart(sp, rsums_done, u.count(1, 1), s_w)
                        wait_apart(sp, rec_in, u.count(64, 0), s_w)
                        sp.dma_start(scratch.rearrange("j g n -> (j g n)").rearrange("(p n) -> p n", p=128),
                                     rsums[:, :]).then_inc(rsums_out, 16)
                    if u := due(at, s, -1, "spread_sums"):
                        wait_apart(sp, rsums_out, u.count(16, 16), s_w)
                        wait_apart(sp, on_done, u.count(1, 0), s_w)
                        for j in range(4):
                            sp.dma_start(rec[32 * j:32 * j + 32, :],
                                         scratch[j].unsqueeze(0).to_broadcast([D, 2, W])).then_inc(rec_in, 16)
                    if u := due(at, s, -3, "store"):
                        wait_apart(sp, fo_done, u.count(1, 1), s_w)
                        sp.dma_start(out_u[u.number()], fo[u.par][:, :, :]).then_inc(stored[u.par], 16)
                    for b in range(NB):
                        if u := due(at, s, 2, "stack", b):
                            stack_parts(u, b)
                    if u := due(at, s, 1, "stack_max"):
                        wait_apart(sp, m3_done, u.count(1, 1), s_w)
                        for n in range(3):
                            sp.dma_start(stack[u.par][KROWS + n:KROWS + n + 1, :, :, 0, :],
                                         mparts[:, n, :]).then_inc(m_stacked[u.par], 16)

            iterations(sp, body, once)
            for p in range(2):
                sp.wait_ge(stored[p], 16 * UNITS // 2)

        @block.gpsimd
        def _(pool):
            nc.gpsimd.memset(minus_half[:, :], -0.5).then_inc(s_half, 1)
            nc.gpsimd.memset(eps_sb[:, :], EPS).then_inc(s_half, 1)
            pool.wait_ge(s_half, 2)

            def once(i):
                if i == -LEAD:
                    for p in range(2):
                        nc.gpsimd.memset(vp[p][:, :, :, D:2 * D], 1.0).then_inc(s_const, 1)
                    for p in range(2):
                        pool.wait_ge(s_const, p + 2)
                        nc.gpsimd.memset(stack[p][KROWS:KROWS + 3, :, :, 1, :], 1.0).then_inc(s_const, 1)
                    pool.wait_ge(s_const, 4)
                    pool.wait_ge(s_w, 16 * 5)

            def inverse_deviation(u, mv, ve, rs, mv_done, ve_done, rs_done, used):
                wait(pool, mv_done, u.count(1, 1))
                wait(pool, used, u.count(1, 0))
                nc.gpsimd.tensor_tensor(ve[:, :], mv[:, :, 1], eps_sb[:, :], ALU.add).then_inc(ve_done, 1)
                wait(pool, ve_done, u.count(1, 1))
                nc.gpsimd.tensor_tensor(rs[:, :], ve[:, :], minus_half[:, :], ALU.pow
                                        ).then_inc(rs_done, 1)

            def low_half(u, f):
                wait(pool, hi_done, u.count(FCH, f + 1))
                wait(pool, proj_mm, u.count(FCH, f + 1 - FCH))
                nc.gpsimd.tensor_tensor(hid_lo[:, f, :, :], hid[f % 2],
                                        hid_hi[:, f, :, :].bitcast(F32), ALU.subtract).then_inc(lo_done, 1)

            def body(at):
                for s in range(SLOTS):
                    if (u := due(at, s, 2, "scaled")) and not vector_splits(u):
                        scale_qk(pool, nc.gpsimd, u)
                    if (u := due(at, s, 2, "rope")) and not vector_splits(u):
                        rotate_qk(pool, nc.gpsimd, u)
                    if (u := due(at, s, 2, "rest1")) and not vector_splits(u):
                        first_rest(pool, nc.gpsimd, u)
                    if (u := due(at, s, 2, "part3")) and not vector_splits(u):
                        last_part(pool, nc.gpsimd, u)
                    if u := due(at, s, 3, "ctx_low"):
                        wait(pool, ca_hi_done, u.count(1, 1))
                        nc.gpsimd.tensor_tensor(ca_lo[:, :, :], ca[u.par][:, :, :],
                                                ca_hi[:, :, :].bitcast(F32), ALU.subtract
                                                ).then_inc(ca_lo_done, 1)
                    if u := due(at, s, 3, "rs1"):
                        inverse_deviation(u, mv1, ve1, rs1, mv1_done, ve1_done, rs1_done, xn_done)
                    for f in range(FCH):
                        if u := due(at, s, -2, "low", f):
                            low_half(u, f)
                    if u := due(at, s, -1, "gated"):
                        wait(pool, oc_in, u.count(64, 64))
                        wait(pool, rec_in, u.count(64, 64))
                        wait(pool, wo_mm, u.count(1, 0))
                        nc.gpsimd.tensor_tensor(on[:, :], oc[:, :], rec[:, :], ALU.mult
                                                ).then_inc(on_done, 1)
                    if u := due(at, s, -1, "x2"):
                        wait(pool, attn_out, u.count(1, 1))
                        wait(pool, xr_in[u.par], u.pair_count(16, 16))
                        wait(pool, fo_done, u.count(1, -1))
                        nc.gpsimd.tensor_tensor(
                            x2[u.par][:, :, :], xr[u.par][:, :, :],
                            attn[:, :].rearrange("p (b t) -> p b t", b=NB), ALU.add
                        ).then_inc(x2_done, 1)
                    if u := due(at, s, -2, "rs2"):
                        inverse_deviation(u, mv2, ve2, rs2, mv2_done, ve2_done, rs2_done, xn2_done)

            iterations(pool, body, once)

        @block.scalar
        def _(act):
            def once(i):
                if i == -LEAD:
                    act.wait_ge(s_small, 16 * 6)
                    nc.scalar.activation(gate_x[:, :], gates[:, 0:1], ACT.Tanh).then_inc(s_gate, 1)
                    nc.scalar.activation(gate_f[:, :], gates[:, 1:2], ACT.Tanh).then_inc(s_gate, 1)
                if i == -1:
                    act.wait_ge(s_split, 2)
                if i == 0:
                    act.wait_ge(s_bias, 1)

            def rectify(u, f):
                wait(act, fc_mm, u.count(FCH, f + 1))
                wait(act, hid_done, u.count(FCH, f - 1))
                nc.scalar.activation(
                    relu[f % 2], (gb, ga, gb, ga)[f][:, :].rearrange("p (n c) -> p n c", n=2),
                    ACT.Relu).then_inc(relu_done, 1)

            def square(u, f):
                wait(act, relu_done, u.count(FCH, f + 1))
                wait(act, lo_done, u.count(FCH, f - 1))
                nc.scalar.activation(hid[f % 2], relu[f % 2], ACT.Square
                                     ).then_inc(hid_done, 1)

            def high_half(u, f):
                wait(act, hid_done, u.count(FCH, f + 1))
                wait(act, proj_mm, u.count(FCH, f + 1 - FCH))
                nc.scalar.activation(hid_hi[:, f, :, :], hid[f % 2], ACT.Copy
                                     ).then_inc(hi_done, 1)

            def body(at):
                for s in range(SLOTS):
                    if u := due(at, s, 3, "ctx_high"):
                        wait(act, c_in[u.par], u.pair_count(16, 16))
                        wait(act, k_mm, u.count(1, 0))
                        nc.scalar.activation(ca_hi[:, :, :], ca[u.par][:, :, :], ACT.Copy
                                             ).then_inc(ca_hi_done, 1)
                    if u := due(at, s, 3, "xn_high"):
                        wait(act, xn_done, u.count(1, 1))
                        wait(act, q_mm, u.count(1, 0))
                        nc.scalar.activation(xn_hi[:, :, :], xn[:, :, :], ACT.Copy
                                             ).then_inc(xn_hi_done, 1)
                    if u := due(at, s, 2, "q_out"):
                        wait(act, q_mm, u.count(1, 1))
                        wait(act, p3_done, u.count(1, -1))
                        nc.scalar.activation(qk[u.par][:, 0, :], ga[:, :], ACT.Identity,
                                             bias=bq_sb[:, :]).then_inc(q_out, 1)
                    if u := due(at, s, 2, "k_out"):
                        wait(act, k_mm, u.count(1, 1))
                        nc.scalar.activation(qk[u.par][:, 1, :], gb[:, :], ACT.Identity,
                                             bias=bk_sb[:, :]).then_inc(k_out, 1)
                    if u := due(at, s, 2, "part1"):
                        wait(act, rope_done, u.count(1, 1))
                        wait(act, q_out, u.count(1, 1))
                        wait(act, k_out, u.count(1, 1))
                        other = Unit(u.r, u.k - 1)
                        for b in range(NB):
                            wait(act, stacked[other.par][b], other.pair_count(96, 96))
                        nc.scalar.activation(parts[:, 0:6:3, :], qk[u.par][:, :, :], ACT.Copy
                                             ).then_inc(p1_done, 1)
                    if u := due(at, s, 2, "part2"):
                        wait(act, r1_done, u.count(1, 1))
                        nc.scalar.activation(parts[:, 1:6:3, :], qk[u.par][:, :, :], ACT.Copy
                                             ).then_inc(p2_done, 1)
                    if u := due(at, s, 1, "v_out"):
                        wait(act, v_mm, u.count(1, 1))
                        wait(act, pv_mm, u.count(GROUPS, -GROUPS))
                        nc.scalar.activation(
                            vp[u.par][:, :, :, 0:D], ga[:, :].rearrange("p (n h i) -> p n h i", h=H, i=D),
                            ACT.Copy).then_inc(v_out, 1)
                    if u := due(at, s, -3, "y_out"):
                        wait(act, proj_mm, u.count(FCH, FCH))
                        wait(act, count_step, u.count(STEPS, 0))
                        nc.scalar.activation(y_sb[:, :], y_bank[:, :], ACT.Copy).then_inc(y_out, 1)
                    if u := due(at, s, -2, "xh"):
                        wait(act, xt_mm, u.count(1, 1))
                        wait(act, fc_mm, u.count(FCH, -FCH))
                        nc.scalar.activation(
                            xh[u.par][:, :, :], ga[:, :].rearrange("p (n c) -> p n c", n=2), ACT.Copy
                        ).then_inc(xh_done, 1)
                    for f in range(FCH):
                        if u := due(at, s, -2, "relu", f):
                            rectify(u, f)
                        if u := due(at, s, -2, "square", f):
                            square(u, f)
                        if u := due(at, s, -2, "high", f):
                            high_half(u, f)
                    if u := due(at, s, -1, "attn"):
                        wait(act, wo_mm, u.count(1, 1))
                        wait(act, x2_done, u.count(1, 0))
                        nc.scalar.activation(attn[:, :], ga[:, :], ACT.Identity,
                                             scale=gate_x[:, :], bias=bias_o[:, :]).then_inc(attn_out, 1)
                    for n in range(ITEMS):
                        if u := due(at, s, 0, "exp", n):
                            wait(act, score_mm, u.count(ITEMS, n + 1))
                            if n % 4 == 0:
                                wait(act, pv_mm, u.count(GROUPS, n // 4 - 1))
                            nc.scalar.activation(
                                probs[:, n % 8, :, :],
                                score_bank[n % 2][:, :].rearrange("p (n t) -> p n t", n=2),
                                ACT.Exp, scale=1.0 / D ** 0.5).then_inc(exp_done, 1)
                    for b in range(NB):
                        if u := due(at, s, 0, "u_out", b):
                            copy_u(u, b)

            def copy_u(u, b):
                wait(act, pv_mm, u.count(GROUPS, 2 * b + 2))
                if b == 0:
                    wait(act, sums_in, u.count(64, 0))
                    wait(act, oc_in, u.count(64, 0))
                nc.scalar.activation(usb[:, :, b, :], u_bank[:, :].rearrange("p (g t) -> p g t", g=2),
                                     ACT.Copy).then_inc(u_out, 1)

            iterations(act, body, once)

        @block.vector
        def _(dve):
            def once(i):
                if i == -LEAD:
                    dve.wait_ge(s_wqk, 32)
                    nc.vector.tensor_copy(wqk_hi[:, :, :], wqk_sb[:, :, :]).then_inc(s_qk, 1)
                    dve.wait_ge(s_qk, 1)
                    nc.vector.tensor_tensor(wqk_lo[:, :, :], wqk_sb[:, :, :],
                                            wqk_hi[:, :, :].bitcast(F32), ALU.subtract).then_inc(s_qk, 1)
                    dve.wait_ge(s_w, 16 * 5)
                if i == -2:
                    dve.wait_ge(s_bvo, 1)
                    dve.wait_ge(s_small, 16 * 6)
                    nc.vector.tensor_tensor(bias_t[:, :], y_bank[:, 0:1], bo_sb[:, :], ALU.add
                                            ).then_inc(s_gscaled, 1)
                    dve.wait_ge(s_gate, 2)
                    dve.wait_ge(s_gscaled, 1)
                    nc.vector.tensor_tensor(bias_o[:, :], bias_t[:, :], gate_x[:, :], ALU.mult
                                            ).then_inc(s_bias, 1)
                    nc.vector.tensor_scalar(gates[:, 1:2], gate_f[:, :], 1.0 / STEPS, None, ALU.mult
                                            ).then_inc(s_gscaled, 1)
                if i == -1:
                    split(wfc_sb, wfc_hi, wfc_lo, 0)
                if i == 0:
                    split(wproj_sb, wproj_hi, wproj_lo, 1)
                    dve.wait_ge(s_gscaled, 2)

            def split(raw, hi, lo, n):
                dve.wait_ge(s_ffn, 32)
                nc.vector.tensor_copy(hi[:, :, :], raw).then_inc(s_split, 1)
                dve.wait_ge(s_split, 2 * n + 1)
                nc.vector.tensor_tensor(lo[:, :, :], raw, hi[:, :, :].bitcast(F32),
                                        ALU.subtract).then_inc(s_split, 1)

            def statistics(u, src, st, mv, st_done, mv_done):
                for b in range(NB):
                    last = nc.vector.bn_stats(st[:, b, :], src[:, b, :])
                last.then_inc(st_done, 1)
                wait(dve, st_done, u.count(1, 1))
                nc.vector.memset(fence[:, :], 0.0)
                for b in range(NB):
                    last = nc.vector.bn_aggr(mv[:, b, :], st[:, b, :])
                last.then_inc(mv_done, 1)

            def normalize(u, dst, src, mv, rs, rs_done, done):
                wait(dve, rs_done, u.count(1, 1))
                for b in range(NB):
                    last = nc.vector.tensor_scalar(dst[:, b, :], src[:, b, :], mv[:, b, 0:1],
                                                   rs[:, b:b + 1], ALU.subtract, ALU.mult)
                last.then_inc(done, 1)

            def count_spikes(u, n):
                y = y_sb[:, :]
                if n == 0:
                    wait(dve, y_out, u.count(1, 1))
                    wait(dve, fo_done, u.count(1, 0))
                    nc.vector.tensor_scalar(cnt[0][:, :], y, thresholds[0], None, ALU.is_gt
                                            ).then_inc(count_step, 1)
                    return
                wait(dve, count_step, u.count(STEPS, n))
                if n < STEPS:
                    nc.vector.scalar_tensor_tensor(
                        out=cnt[n % 2][:, :], in0=y, scalar=thresholds[n],
                        in1=cnt[(n - 1) % 2][:, :], op0=ALU.is_gt, op1=ALU.add).then_inc(count_step, 1)
                    return
                wait(dve, stored[u.par], u.pair_count(16, 0))
                nc.vector.scalar_tensor_tensor(
                    out=fo[u.par][:, :, :],
                    in0=cnt[(STEPS - 1) % 2][:, :].rearrange("p (b t) -> p b t", b=NB),
                    scalar=gates[:, 1:2], in1=x2[u.par][:, :, :], op0=ALU.mult, op1=ALU.add
                ).then_inc(fo_done, 1)

            def max_parts(u):
                wait(dve, mt_mm, u.count(1, 1))
                other = Unit(u.r, u.k - 1)
                wait(dve, m_stacked[other.par], other.pair_count(48, 48))
                m = gb[0:ITEMS, 0:T]
                nc.vector.tensor_copy(mparts[:, 0, :], m).then_inc(m1_done, 1)
                wait(dve, m1_done, u.count(1, 1))
                nc.vector.tensor_tensor(mrest[:, :], m, mparts[:, 0, :], ALU.subtract
                                        ).then_inc(mr_done, 1)
                wait(dve, mr_done, u.count(1, 1))
                nc.vector.tensor_copy(mparts[:, 1, :], mrest[:, :]).then_inc(m2_done, 1)
                wait(dve, m2_done, u.count(1, 1))
                nc.vector.tensor_tensor(mparts[:, 2, :], mrest[:, :], mparts[:, 1, :],
                                        ALU.subtract).then_inc(m3_done, 1)

            def body(at):
                for s in range(SLOTS):
                    if u := due(at, s, -1, "recip"):
                        wait(dve, sums_in, u.count(64, 64))
                        wait(dve, rsums_out, u.count(16, 0))
                        nc.vector.reciprocal(rsums[:, :], sums[:, :]).then_inc(rsums_done, 1)
                    for n in range(ITEMS):
                        if u := due(at, s, 1, "take_max", n):
                            if n == 0:
                                wait(dve, mt_mm, u.count(1, -1))
                            wait(dve, max_mm, u.count(ITEMS, n + 1))
                            nc.vector.tensor_reduce(
                                mx[u.par][:, :, n // H, n % H],
                                max_bank[n % 2][:, :].rearrange("p (n t) -> p n t", n=2),
                                AX.X, ALU.max, negate=True).then_inc(max_done, 1)
                    if u := due(at, s, 1, "max_parts"):
                        max_parts(u)
                    for n, (src, dst) in enumerate(((H * ROT // 2, 0), (0, H * ROT // 2))):
                        if u := due(at, s, 2, "turned", n):
                            half = H * ROT // 2
                            if n == 0:
                                wait(dve, q_out, u.count(1, 1))
                                wait(dve, k_out, u.count(1, 1))
                                wait(dve, rope_done, u.count(1, 0))
                            nc.vector.tensor_tensor(
                                turned[dst:dst + half, :, :].rearrange("p n (b t) -> p (n b) t", b=NB),
                                qk[u.par][src:src + half, :, :].rearrange("p n (b t) -> p (n b) t", b=NB),
                                sin_sb[src:src + half, :].unsqueeze(1).to_broadcast([half, 2 * NB, T]),
                                ALU.mult).then_inc(turned_done, 1)
                    if (u := due(at, s, 2, "scaled")) and vector_splits(u):
                        scale_qk(dve, nc.vector, u)
                    if (u := due(at, s, 2, "rope")) and vector_splits(u):
                        rotate_qk(dve, nc.vector, u)
                    if (u := due(at, s, 2, "rest1")) and vector_splits(u):
                        first_rest(dve, nc.vector, u)
                    if (u := due(at, s, 2, "part3")) and vector_splits(u):
                        last_part(dve, nc.vector, u)
                    if u := due(at, s, -2, "stats2"):
                        wait(dve, x2_done, u.count(1, 1))
                        wait(dve, xn2_done, u.count(1, 0))
                        statistics(u, x2[u.par], st2, mv2, st2_done, mv2_done)
                    if u := due(at, s, -2, "norm2"):
                        wait(dve, xt_mm, u.count(1, 0))
                        normalize(u, xn2, x2[u.par], mv2, rs2, rs2_done, xn2_done)
                    if u := due(at, s, -2, "xl"):
                        wait(dve, xh_done, u.count(1, 1))
                        nc.vector.tensor_tensor(
                            xl[u.par][:, :, :], ga[:, :].rearrange("p (n c) -> p n c", n=2),
                            xh[u.par][:, :, :].bitcast(F32), ALU.subtract).then_inc(xl_done, 1)
                    for n in range(STEPS + 1):
                        if u := due(at, s, -3, "count", n):
                            count_spikes(u, n)
                    if u := due(at, s, 3, "stats1"):
                        wait(dve, x_in[u.par], u.pair_count(16, 16))
                        wait(dve, xn_done, u.count(1, 0))
                        statistics(u, xa[u.par], st1, mv1, st1_done, mv1_done)
                    if u := due(at, s, 3, "norm1"):
                        wait(dve, xn_lo_done, u.count(1, 0))
                        normalize(u, xn, xa[u.par], mv1, rs1, rs1_done, xn_done)
                    if u := due(at, s, 3, "xn_low"):
                        wait(dve, xn_hi_done, u.count(1, 1))
                        nc.vector.tensor_tensor(xn_lo[:, :, :], xn[:, :, :], xn_hi[:, :, :].bitcast(F32),
                                                ALU.subtract).then_inc(xn_lo_done, 1)

            iterations(dve, body, once)

        @block.tensor
        def _(pe):
            def once(i):
                if i == -LEAD:
                    pe.wait_ge(s_qk, 2)
                if i == -2:
                    pe.wait_ge(s_w, 16 * 5)
                    pe.wait_ge(s_small, 16 * 6)
                    nc.tensor.matmul(y_bank[:, 0:1], wo_sb[:, :], bv_sb[:, :], start=True, stop=True
                                     ).then_inc(s_bvo, 1)
                if i == -1:
                    pe.wait_ge(s_const, 4)
                if i == 1:
                    pe.wait_ge(s_split, 4)
                    pe.wait_ge(s_gscaled, 2)

            def wait_peeled(u, sem, value):
                if u.fixed:
                    wait(pe, sem, value)

            def other(u, ahead):
                return Unit(u.r, u.k + ahead)

            def project(dst, n, hi, lo):
                for m, (w, xx) in enumerate(((wqk_hi, hi), (wqk_hi, lo), (wqk_lo, hi))):
                    last = nc.tensor.matmul(dst[:, :], w[:, n, :], xx[:, :, :].rearrange("c b t -> c (b t)"),
                                            start=(m == 0), stop=(m == 2))
                return last

            def project_q(u):
                wait(pe, xn_lo_done, u.count(1, 1))
                wait(pe, attn_out, other(u, -4).count(1, 1))
                wait_peeled(u, relu_done, other(u, -5).count(FCH, FCH))
                wait_peeled(u, v_out, other(u, -2).count(1, 1))
                project(ga, 0, xn_hi, xn_lo).then_inc(q_mm, 1)

            def project_k(u):
                wait(pe, ca_lo_done, u.count(1, 1))
                wait(pe, mr_done, other(u, -2).count(1, 1))
                wait_peeled(u, k_out, other(u, -1).count(1, 1))
                project(gb, 1, ca_hi, ca_lo).then_inc(k_mm, 1)

            def project_v(u):
                p = u.par
                wait(pe, q_out, other(u, 1).count(1, 1))
                wait_peeled(u, attn_out, other(u, -3).count(1, 1))
                wait_peeled(u, relu_done, other(u, -4).count(FCH, FCH))
                wait(pe, c_in[p], u.pair_count(16, 16))
                for n in range(2 * NB):
                    last = nc.tensor.matmul(ga[:, n * C:(n + 1) * C],
                                            ca[p][:, n // 2, (n % 2) * 128:(n % 2) * 128 + 128],
                                            wv_sb[:, :], start=True, stop=True)
                last.then_inc(v_mm, 1)

            def project_out(u):
                wait(pe, on_done, u.count(1, 1))
                wait(pe, relu_done, other(u, -1).count(FCH, FCH))
                wait_peeled(u, v_out, other(u, 2).count(1, 1))
                nc.tensor.matmul(ga[:, :], wo_sb[:, :], on[:, :], start=True, stop=True).then_inc(wo_mm, 1)

            def turn(u):
                wait(pe, xn2_done, u.count(1, 1))
                wait(pe, v_out, other(u, 3).count(1, 1))
                wait_peeled(u, attn_out, u.count(1, 1))
                wait_peeled(u, relu_done, other(u, -1).count(FCH, FCH))
                for dc in range(2):
                    for b in range(NB):
                        o = (dc * NB + b) * 128
                        last = nc.tensor.transpose(ga[:, o:o + 128], xn2[:, b, dc * 128:(dc + 1) * 128],
                                                   eye_sb[:, :])
                last.then_inc(xt_mm, 1)

            def turn_max(u):
                wait(pe, max_done, u.count(ITEMS, ITEMS))
                wait(pe, relu_done, other(u, -3).count(FCH, 3))
                wait_peeled(u, k_out, other(u, 1).count(1, 1))
                for half in range(2):
                    last = nc.tensor.transpose(gb[0:ITEMS, half * 128:half * 128 + 128],
                                               mx[u.par][:, half, :, :].rearrange("p b h -> p (b h)"),
                                               eye_sb[:, :])
                last.then_inc(mt_mm, 1)

            def max_item(u, n):
                b, h = n // H, n % H
                q, k = stack[u.par][:, b, h, 0, :], stack[u.par][:, b, h, 1, :]
                if h == 0:
                    wait(pe, stacked[u.par][b], u.pair_count(96, 96))
                wait(pe, max_done, u.count(ITEMS, n - 1))
                for half in range(2):
                    last = nc.tensor.matmul(max_bank[n % 2][:, half * T:(half + 1) * T],
                                            q[0:KROWS, half * 128:half * 128 + 128], k[0:KROWS, :],
                                            start=True, stop=True)
                last.then_inc(max_mm, 1)

            def score_item(u, n):
                b, h = n // H, n % H
                q, k = stack[u.par][:, b, h, 0, :], stack[u.par][:, b, h, 1, :]
                if n == 0:
                    wait(pe, m_stacked[u.par], u.pair_count(48, 48))
                wait(pe, exp_done, u.count(ITEMS, n - 1))
                for half in range(2):
                    last = nc.tensor.matmul(score_bank[n % 2][:, half * T:(half + 1) * T],
                                            k[0:KROWS + 3, half * 128:half * 128 + 128],
                                            q[0:KROWS + 3, :], start=True, stop=True)
                last.then_inc(score_mm, 1)

            def v_products(u, g):
                b, top = g // 2, g % 2
                wait(pe, exp_done, u.count(ITEMS, 4 * g + 4))
                if g == 0:
                    wait(pe, v_out, u.count(1, 1))
                if top == 0:
                    wait(pe, u_out, u.count(2, b))
                for half in range(2):
                    for j in range(4):
                        last = nc.tensor.matmul(
                            u_bank[32 * j:32 * j + 32, top * T:(top + 1) * T],
                            vp[u.par][:, 2 * b + half, 4 * top + j, :],
                            probs[:, (4 * g + j) % 8, half, :], start=(half == 0), stop=(half == 1))
                last.then_inc(pv_mm, 1)

            def first_product(u, f):
                p = u.par
                if f == 0:
                    wait(pe, xl_done, u.count(1, 1))
                    wait(pe, k_out, other(u, 4).count(1, 1))
                    wait_peeled(u, mr_done, other(u, 2).count(1, 1))
                    wait_peeled(u, relu_done, u.count(FCH, 0))
                if f == 2:
                    wait(pe, relu_done, u.count(FCH, 1))
                if f == 3:
                    wait(pe, relu_done, u.count(FCH, 2))
                dst = (gb, ga, gb, ga)[f]
                for half in range(2):
                    f0 = (2 * f + half) * 128
                    n = 0
                    for dc in range(2):
                        for w, xx in ((wfc_hi, xh), (wfc_hi, xl), (wfc_lo, xh)):
                            last = nc.tensor.matmul(dst[:, half * 256:half * 256 + 256],
                                                    w[:, dc, f0:f0 + 128], xx[p][:, dc, :],
                                                    start=(n == 0), stop=(n == 5))
                            n += 1
                last.then_inc(fc_mm, 1)

            def second_product(u, f, half):
                if half == 0:
                    wait(pe, lo_done, u.count(FCH, f + 1))
                    if f == 0:
                        wait(pe, y_out, u.count(1, 0))
                for b in range(NB):
                    for n, (hh, w) in enumerate(((hid_hi, wproj_hi), (hid_lo, wproj_hi), (hid_hi, wproj_lo))):
                        last = nc.tensor.matmul(
                            y_bank[:, b * T:(b + 1) * T], hh[:, f, half, b * C:(b + 1) * C],
                            w[:, 2 * f + half, :], start=(f == 0 and half == 0 and b == 0 and n == 0),
                            stop=(f == FCH - 1 and half == 1 and n == 2), skip_group_check=True)
                if half == 1:
                    last.then_inc(proj_mm, 1)

            def body(at):
                for s in range(SLOTS):
                    for n in range(ITEMS):
                        if u := due(at, s, 1, "max", n):
                            max_item(u, n)
                    for n in range(ITEMS):
                        if u := due(at, s, 0, "score", n):
                            score_item(u, n)
                    for g in range(GROUPS):
                        if u := due(at, s, 0, "v_product", g):
                            v_products(u, g)
                    for ahead, step, product in ((2, "q", project_q), (2, "k", project_k),
                                                 (1, "v", project_v), (-2, "turn", turn)):
                        if u := due(at, s, ahead, step):
                            product(u)
                    for f in range(FCH):
                        if u := due(at, s, -2, "fc", f):
                            first_product(u, f)
                    for n in range(2 * FCH):
                        if u := due(at, s, -2, "proj", n):
                            second_product(u, n // 2, n % 2)
                    for ahead, step, product in ((-1, "wo", project_out), (1, "turn_max", turn_max)):
                        if u := due(at, s, ahead, step):
                            product(u)

            iterations(pe, body, once)


_NAMES = ("x", "ctx", "gx", "gf", "wq", "wk", "wv", "wo", "bq", "bk", "bv", "bo", "wfc", "wproj",
          "cos", "sin", "eye")


def kernel(x, ctx_1024, g_xattn, g_ffn, L0_xattn_Wq, L0_xattn_bq, L0_xattn_Wk, L0_xattn_bk,
           L0_xattn_Wv, L0_xattn_bv, L0_xattn_Wo, L0_xattn_bo, L0_ffn_W_fc, L0_ffn_W_proj):
    import concourse.bacc as bacc
    from concourse.bass_utils import run_bass_kernel_spmd as run

    order = np.arange(C).reshape(H, D).T.reshape(-1)
    out_order = np.arange(C).reshape(2, 4, D).transpose(1, 2, 0).reshape(-1)
    wq, wk, wv, wo = (np.asarray(w) for w in (L0_xattn_Wq, L0_xattn_Wk, L0_xattn_Wv, L0_xattn_Wo))

    theta = (1.0 / np.float32(2500) ** (np.arange(0, ROT, 2, dtype=np.float32) / np.float32(ROT))
             ).astype(np.float32)
    angle = np.arange(T, dtype=np.float32)[None, :] * theta[:, None]
    cos = np.repeat(np.cos(angle), H, axis=0)
    sin = np.repeat(np.sin(angle), H, axis=0)
    arrays = {
        "x": np.asarray(x), "ctx": np.asarray(ctx_1024), "gx": np.asarray(g_xattn), "gf": np.asarray(g_ffn),
        "wq": wq[order].T, "wk": wk[order].T, "wv": wv.T, "wo": wo.T[out_order],
        "bq": np.asarray(L0_xattn_bq)[order], "bk": np.asarray(L0_xattn_bk)[order],
        "bv": np.asarray(L0_xattn_bv)[out_order], "bo": np.asarray(L0_xattn_bo),
        "wfc": np.asarray(L0_ffn_W_fc).T, "wproj": np.asarray(L0_ffn_W_proj).T,
        "cos": np.concatenate([cos, cos]), "sin": np.concatenate([sin, -sin]),
        "eye": np.eye(128, dtype=np.float32),
    }
    arrays = {f"in_{n}": np.ascontiguousarray(arrays[n], dtype=np.float32) for n in _NAMES}
    nc = bacc.Bacc("TRN2", target_bir_lowering=False, num_devices=1)
    args = [nc.dram_tensor(n, a.shape, F32, kind="ExternalInput").ap() for n, a in arrays.items()]
    out = nc.dram_tensor("out_0", (B, C, T), F32, kind="ExternalOutput").ap()
    scratch = nc.dram_tensor("scratch", (4, 2, W), F32, kind="Internal").ap()
    build(nc, *args, out, scratch)
    r = run(nc, [arrays], core_ids=[0])
    return r.results[0]["out_0"]
```
